# Optimizing a Trainium2 kernel written in Bass

```python
import numpy as np
import jax
import jax.numpy as jnp

def _softmax(x, axis=-1):
    return jax.nn.softmax(x, axis=axis)

def _gelu(x):
    return jax.nn.gelu(x, approximate=True)

def _silu(x):
    return jax.nn.silu(x)

def _sigmoid(x):
    return jax.nn.sigmoid(x)

def _layernorm(x, axis=-1, eps=1e-05):
    m = jnp.mean(x, axis=axis, keepdims=True)
    v = jnp.var(x, axis=axis, keepdims=True)
    return (x - m) / jnp.sqrt(v + eps)

def _scatter_add(tgt, idx, src, axis=0):
    return tgt.at[idx].add(src)

def _segment_sum(src, seg, n):
    return jax.ops.segment_sum(src, seg, n)
kernel_name = 'mk_gnn_resnorm_d1_gnn_r8_1a9384'

def setup_inputs(seed: int=0):
    np.random.seed(seed)
    _w = jnp.asarray

    def _rec_inputs():
        import jax
        import jax.numpy as jnp
        _gk = jax.random.key(seed)
        x = -0.0006008 + 1.001 * jax.random.normal(jax.random.fold_in(_gk, 1), (6250, 128), jnp.float32)
        _s = jax.random.randint(jax.random.fold_in(_gk, 2), (50000,), 0, 6250, jnp.int32)
        _d = jax.random.randint(jax.random.fold_in(_gk, 3), (50000,), 0, 6250, jnp.int32)
        _loop = jnp.arange(6250, dtype=jnp.int32)
        src = jnp.concatenate([_s, _d, _loop])
        dst = jnp.concatenate([_d, _s, _loop])
        _o = jnp.argsort(dst, stable=True)
        src = src[_o]
        dst = dst[_o]
        edge_attr_128 = 0.000167468 + 1.0002 * jax.random.normal(jax.random.fold_in(_gk, 11), (106250, 128), jnp.float32)
        return (x, src, dst, edge_attr_128)
    x, src, dst, edge_attr_128 = _rec_inputs()

    def _L0_gnn_setup():
        import jax, jax.numpy as jnp
        import numpy as np
        N_NODES = 2500
        N_EDGES = 40000
        D = 128
        LN_EPS = 1e-05
        key = jax.random.key(seed)
        k1, k2, k3, k4 = jax.random.split(key, 4)
        x = jax.random.normal(k1, (N_NODES, D), dtype=jnp.float32)
        edge_index = jax.random.randint(k2, (2, N_EDGES), 0, N_NODES, dtype=jnp.int64)
        edge_attr = jax.random.normal(k3, (N_EDGES, D), dtype=jnp.float32)
        W = jax.random.normal(k4, (3 * D, D), dtype=jnp.float32) / np.sqrt(3 * D)
        b = jnp.zeros((D,), dtype=jnp.float32)
        gamma = jnp.ones((D,), dtype=jnp.float32)
        beta = jnp.zeros((D,), dtype=jnp.float32)
        return {'x': x, 'edge_index': edge_index, 'edge_attr': edge_attr, 'W': W, 'b': b, 'gamma': gamma, 'beta': beta}
    _L0_gnn_all = _L0_gnn_setup()
    _L0_gnn_in = {k: v for k, v in _L0_gnn_all.items() if k in ('W', 'b', 'gamma', 'beta')}
    del _L0_gnn_all
    return {'x': x, 'src': src, 'dst': dst, 'edge_attr_128': edge_attr_128, 'L0_gnn_W': _L0_gnn_in['W'], 'L0_gnn_b': _L0_gnn_in['b'], 'L0_gnn_gamma': _L0_gnn_in['gamma'], 'L0_gnn_beta': _L0_gnn_in['beta']}

def reference(x, src, dst, edge_attr_128, L0_gnn_W, L0_gnn_b, L0_gnn_gamma, L0_gnn_beta):
    import jax
    import jax.numpy as jnp

    def _L0_gnn_ref(x, edge_index, edge_attr, W, b, gamma, beta):
        import jax, jax.numpy as jnp
        import numpy as np
        N_NODES = 2500
        N_EDGES = 40000
        D = 128
        LN_EPS = 1e-05
        row, col = (edge_index[0], edge_index[1])
        msg_in = jnp.concatenate([x[row], x[col], edge_attr], axis=-1)
        h = msg_in @ W + b
        mu = jnp.mean(h, axis=-1, keepdims=True)
        var = jnp.mean(jnp.square(h - mu), axis=-1, keepdims=True)
        h = (h - mu) * jax.lax.rsqrt(var + LN_EPS) * gamma + beta
        msg = jax.nn.relu(h)
        out = jax.ops.segment_sum(msg, row, num_segments=x.shape[0])
        return out
    edge_index = jnp.stack([src, dst])
    x = _layernorm(x + _L0_gnn_ref(x, edge_index, edge_attr_128, L0_gnn_W, L0_gnn_b, L0_gnn_gamma, L0_gnn_beta), axis=-1)
    return x

_drawn_inputs = setup_inputs


def setup_inputs(seed=0):
    import zlib

    import numpy as np

    out = dict(_drawn_inputs(seed))
    spreads = {'L0_gnn_b': (0.0, 0.1), 'L0_gnn_gamma': (1.0, 0.2), 'L0_gnn_beta': (0.0, 0.1)}
    factors = {}
    for name, (base, spread) in spreads.items():
        noise = np.random.default_rng([zlib.crc32(name.encode()), seed]).standard_normal(out[name].shape)
        drawn = base * np.exp(spread * noise) if base else spread * noise
        out[name] = jnp.asarray(drawn.astype(out[name].dtype))
    for name, factor in factors.items():
        out[name] = (out[name] * factor).astype(out[name].dtype)
    return out
```

```python
from contextlib import ExitStack

import concourse.bass as bass
from concourse import mybir

ALU = mybir.AluOpType
ACT = mybir.ActivationFunctionType
AX = mybir.AxisListType
F32 = mybir.dt.float32
BF16 = mybir.dt.bfloat16
I32 = mybir.dt.int32

P = 128
D = 128
TILES = 4
GROUP = TILES * P
EPS = 1e-5
ACCS = TILES

C_ID, C_POW, C_THR, C_IOTA, C_DUMP, C_END = 0, P, P + 2, P + 4, P + 5, P + 6


def shapes(nodes, edges):
    rows = -(-nodes // P)
    pairs = -(-edges // (2 * GROUP))
    return rows, pairs


def constants(nodes):
    import numpy as np
    c = np.zeros((P, C_END), np.float32)
    c[:, C_ID:C_ID + P] = np.eye(P)
    p = np.arange(P)
    low = p < P // 2
    c[:, C_POW] = np.where(low, 4.0 ** (p - 32.0), 0)
    c[:, C_POW + 1] = np.where(low, 0, 4.0 ** (p - 96.0))
    c[:, C_THR] = np.where(low, 2 * 4.0 ** (p - 32.0), 3e38)
    c[:, C_THR + 1] = np.where(low, 2.0 ** -100, 2 * 4.0 ** (p - 96.0))
    c[:, C_IOTA] = p
    c[:, C_DUMP] = shapes(nodes, P)[0] * P + p
    return c


def gnn_kernel(nc, x, src, dst, edge, W, b, gamma, beta, consts, out):
    N, E = x.shape[0], edge.shape[0]
    R, PAIRS = shapes(N, E)
    NPAD = P * R
    AROWS = NPAD + P
    WIN_MAX = NPAD - P
    FULLP, LASTR = N // R, N % R
    LASTE = E - (PAIRS - 1) * 2 * GROUP
    TAIL = LASTE - GROUP
    assert 0 < TAIL <= GROUP and PAIRS > 2 and PAIRS <= P
    RW = R * D
    HALF = 112

    xa_rows = nc.dram_tensor("xa_rows", [NPAD, D], F32, kind="Internal").ap()
    xb_rows = nc.dram_tensor("xb_rows", [NPAD, D], F32, kind="Internal").ap()
    acc = [nc.dram_tensor(f"acc{k}", [AROWS, D], F32, kind="Internal").ap() for k in range(ACCS)]

    with ExitStack() as ctx:
        def sb(name, shape, dt=F32):
            return ctx.enter_context(nc.sbuf_tensor(name, shape, dt))

        def ps(name, shape, dt=F32):
            return ctx.enter_context(nc.psum_tensor(name, shape, dt))

        def sem(name):
            return ctx.enter_context(nc.semaphore(name))

        big = sb("big", [P, ACCS, AROWS])
        con = sb("con", [P, C_END])
        ident_h = sb("ident_h", [P, P], BF16)
        ones = sb("ones", [P, P])
        w = sb("w", [P, 3, D])
        wmean = sb("wmean", [P, 4])
        bias2 = sb("bias2", [P, 2, D])
        gamma_b = sb("gamma_b", [P, D])
        beta_b = sb("beta_b", [P, D])
        eps = sb("eps", [P, 1])
        ids_i = sb("ids_i", [P, 2, 2 * GROUP], I32)
        ids_f = sb("ids_f", [P, 2, 2 * GROUP])
        low_i = sb("low_i", [P, 2, 2 * GROUP], I32)
        low_h = sb("low_h", [P, 2, 2 * GROUP], BF16)
        high_h = sb("high_h", [P, 2, 2 * GROUP], BF16)
        src_f = sb("src_f", [P, PAIRS, 2, TILES])
        src_i = sb("src_i", [P, PAIRS, 2, TILES], I32)
        dst_i = sb("dst_i", [P, PAIRS, 2, TILES], I32)
        to_dump = sb("to_dump", [P, PAIRS, 2, TILES])
        span = sb("span", [P, 4, 2])
        diag = sb("diag", [P, 3, 2, P])
        win_f = sb("win_f", [P, PAIRS, 2])
        win_i = sb("win_i", [P, 2, 2, PAIRS], I32)
        x_now = sb("x_now", [P, 2, D])
        xT = sb("xT", [P, 2, P])
        ea = sb("ea", [P, 2, TILES, D])
        eaT = sb("eaT", [P, 2, TILES, P])
        window = sb("window", [P, 2, D])
        same = sb("same", [P, 2, TILES, P])
        hot = sb("hot", [P, 2, TILES, P])
        gat = sb("gat", [P, 2, TILES, D])
        squared = sb("squared", [P, 2, TILES, D], BF16)
        squares = sb("squares", [P, 2, TILES])
        std = sb("std", [P, 2, TILES])
        rstd = sb("rstd", [P, 2, TILES])
        msg = sb("msg", [P, 2, TILES, D])
        summed = sb("summed", [P, 2, TILES, D])
        over = sb("over", [P, TILES, 2])
        dup = sb("dup", [P, TILES])
        shift = sb("shift", [P, TILES])
        src_now = [sb(f"src_now{s}", [P, TILES], I32) for s in range(2)]
        dst_now = [sb(f"dst_now{s}", [P, TILES], I32) for s in range(2)]
        row_now = [sb(f"row_now{s}", [P, TILES], I32) for s in range(2)]
        mean = sb("mean", [P, R])
        var = sb("var", [P, R])
        sdev = sb("sdev", [P, R])
        rdev = sb("rdev", [P, R])

        pT = ps("pT", [P, TILES, P])
        pS = ps("pS", [P, GROUP])
        pD = ps("pD", [P, GROUP])
        pH = [ps(f"pH{s}", [P, TILES, D]) for s in range(2)]
        pM = ps("pM", [P, TILES, D])
        pW = ps("pW", [P, TILES, 2])

        ident = con[:, C_ID:C_ID + P]
        x_sb = big[:, 0, :]
        zeros = big[:, 3, :]

        con_in = sem("con_in")
        small_in = sem("small_in")
        x_in = sem("x_in")
        ids_in = sem("ids_in")
        pads_set = sem("pads_set")
        dve_step = sem("dve_step")
        prep_ready = sem("prep_ready")
        prep_pe = sem("prep_pe")
        windows_ready = sem("windows_ready")
        x_placed = sem("x_placed")
        x_turned = sem("x_turned")
        xT_copied = sem("xT_copied")
        node_done = sem("node_done")
        node_kept = sem("node_kept")
        tables_out = sem("tables_out")
        acc_set = sem("acc_set")
        ea_in = [sem(f"ea_in{s}") for s in range(2)]
        window_in = [sem(f"window_in{s}") for s in range(2)]
        gat_in = [sem(f"gat_in{s}") for s in range(2)]
        outside_in = sem("outside_in")
        settled = sem("settled")
        acc_added = [sem(f"acc_added{k}") for k in range(ACCS)]
        gather_go = sem("gather_go")
        scatter_go = sem("scatter_go")
        ids_ready = sem("ids_ready")
        ea_turned = sem("ea_turned")
        eaT_copied = sem("eaT_copied")
        src_spread = sem("src_spread")
        dst_spread = sem("dst_spread")
        same_built = sem("same_built")
        hot_built = sem("hot_built")
        weighed = sem("weighed")
        over_found = sem("over_found")
        dup_found = sem("dup_found")
        shift_found = sem("shift_found")
        rows_ready = sem("rows_ready")
        h_ready = sem("h_ready")
        squares_done = sem("squares_done")
        std_ready = sem("std_ready")
        rstd_ready = sem("rstd_ready")
        scaled = sem("scaled")
        z_ready = sem("z_ready")
        msg_ready = sem("msg_ready")
        combined = sem("combined")
        summed_ready = sem("summed_ready")
        CH = 7
        assert R % CH == 0
        CHUNKS = R // CH
        back_in = [sem(f"back_in{c}") for c in range(CHUNKS)]
        half_sum = sem("half_sum")
        centred = sem("centred")
        fin_squares = sem("fin_squares")
        fin_var = sem("fin_var")
        fin_std = sem("fin_std")
        fin_done = sem("fin_done")
        stored = sem("stored")

        def past(at, n):
            return not isinstance(at, int) or at >= n

        def run_pairs(eng, step):
            for s in range(2):
                step(0, s)
            with eng.Fori(1, PAIRS - 1) as q:
                for s in range(2):
                    step(q, s)
            for s in range(2):
                step(PAIRS - 1, s)

        def after(q, s):
            if s == 0:
                return q, 1
            if isinstance(q, int) and q == PAIRS - 1:
                return None
            return q + 1, 0

        def before(q, s):
            if s == 1:
                return q, 0
            if isinstance(q, int) and q == 0:
                return None
            return q - 1, 1

        def node_steps(eng, step):
            step(0, 0)
            step(1, 1)
            with eng.Fori(1, R // 2) as i:
                step(2 * i, 0)
                step(2 * i + 1, 1)
            if R % 2:
                step(R - 1, 0)

        block = ctx.enter_context(nc.Block())

        @block.sync
        def _(sp):
            sp.dma_start(con[:], consts).then_inc(con_in, 16)
            sp.dma_start(w[:], W.rearrange("(c k) n -> k c n", k=P)).then_inc(small_in, 16)
            for row, to in ((b, bias2[:, 0, :]), (gamma, gamma_b[:]), (beta, beta_b[:])):
                sp.dma_start(to, row.rearrange("(a d) -> a d", a=1).to_broadcast([P, D])).then_inc(small_in, 16)
            sp.wait_ge(pads_set, 1)
            for a, z in ((0, HALF), (HALF, FULLP)):
                sp.dma_start(x_sb[a:z, 0:RW], x[a * R:z * R, :].rearrange("(p j) d -> p (j d)", j=R)).then_inc(x_in, 16)
            sp.dma_start(x_sb[FULLP:FULLP + 1, 0:LASTR * D],
                         x[FULLP * R:N, :].rearrange("(p j) d -> p (j d)", p=1)).then_inc(x_in, 16)
            sp.wait_ge(pads_set, 2)
            full = PAIRS - 1
            for n, ids in enumerate((src, dst)):
                for a, z in ((0, full // 16 * 16), (full // 16 * 16, full)):
                    sp.dma_start(ids_i[a:z, n, :], ids[a * 2 * GROUP:z * 2 * GROUP].rearrange("(p e) -> p e", e=2 * GROUP)
                                 ).then_inc(ids_in, 16)
                sp.dma_start(ids_i[full:full + 1, n, 0:LASTE],
                             ids[full * 2 * GROUP:E].rearrange("(p e) -> p e", p=1)).then_inc(ids_in, 16)
            sp.dma_start(acc[0][0:N, :], x).then_inc(acc_set, 16)
            sp.wait_ge(pads_set, 3)
            sp.dma_start(acc[0][N:AROWS, :].rearrange("(p j) d -> p (j d)", j=2),
                         zeros[0:(AROWS - N) // 2, 0:2 * D]).then_inc(acc_set, 16)
            for k in range(1, ACCS):
                sp.dma_start(acc[k].rearrange("(p j) d -> p (j d)", p=P), zeros).then_inc(acc_set, 16)
            sp.wait_ge(node_kept, R)
            for n, t in enumerate((xa_rows, xb_rows)):
                sp.dma_start(t.rearrange("(p j) d -> p (j d)", p=P), big[:, 1 + n, 0:RW]).then_inc(tables_out, 16)
            sp.wait_ge(tables_out, 32)
            sp.wait_ge(windows_ready, 1)

            def step(q, s):
                g = 2 * q + s
                if past(g, 2):
                    sp.wait_ge(ea_turned, g - 1)
                if isinstance(q, int) and g == 2 * PAIRS - 1:
                    at, pt = g * GROUP, TAIL // TILES
                    sp.dma_start(ea[0:pt, s, :, :], edge[at:at + pt * TILES, :].rearrange("(p k) d -> p k d", k=TILES)
                                 ).then_inc(ea_in[s], 16)
                    if TAIL % TILES:
                        sp.dma_start(ea[pt:pt + 1, s, 0:TAIL % TILES, :],
                                     edge[at + pt * TILES:E, :].rearrange("(p k) d -> p k d", p=1)).then_inc(ea_in[s], 16)
                else:
                    sp.dma_start(ea[:, s, :, :], edge[bass.ds(g * GROUP, GROUP), :].rearrange("(p k) d -> p k d", k=TILES)
                                 ).then_inc(ea_in[s], 16)
                if past(g, 2):
                    sp.wait_ge(h_ready, g - 1)
                start = sp.value_load(win_i[0:1, 0, s, bass.ds(q, 1)], min_val=0, max_val=WIN_MAX)
                sp.dma_start(window[:, s, :], xb_rows[bass.ds(start, P), :]).then_inc(window_in[s], 16)

            run_pairs(sp, step)
            for k in range(ACCS):
                sp.wait_ge(acc_added[k], 16 * 2 * PAIRS)
            for c in range(CHUNKS):
                for k in range(ACCS):
                    sp.dma_start(big[:, k, c * CH * D:(c + 1) * CH * D],
                                 acc[k][0:NPAD, :].rearrange("(p j) d -> p j d", p=P)[:, c * CH:(c + 1) * CH, :]
                                 .rearrange("p j d -> p (j d)")).then_inc(back_in[c], 16)
            n = 0
            for c in range(CHUNKS):
                sp.wait_ge(fin_done, c + 1)
                j0, j1 = c * CH, (c + 1) * CH
                head = out[0:FULLP * R, :].rearrange("(p j) d -> p j d", j=R)
                for a, z in ((0, HALF), (HALF, FULLP)):
                    sp.dma_start(head[a:z, j0:j1, :], big[a:z, 0, j0 * D:j1 * D].rearrange("p (j d) -> p j d", d=D)
                                 ).then_inc(stored, 16)
                    n += 1
                if j0 < LASTR:
                    m = min(j1, LASTR)
                    sp.dma_start(out[FULLP * R + j0:FULLP * R + m, :].rearrange("(p j) d -> p j d", p=1),
                                 big[FULLP:FULLP + 1, 0, j0 * D:m * D].rearrange("p (j d) -> p j d", d=D)).then_inc(stored, 16)
                    n += 1
            sp.wait_ge(stored, 16 * n)

        @block.gpsimd
        def _(pool):
            pool.memset(x_sb, 0.0).then_inc(pads_set, 1)
            pool.memset(ids_i[:, 0, :], NPAD - 1)
            pool.memset(ids_i[:, 1, :], N - 1).then_inc(pads_set, 1)
            pool.memset(zeros, 0.0).then_inc(pads_set, 1)

            def place(j, slot):
                if past(j, 2):
                    pool.wait_ge(x_turned, j - 1)
                pool.tensor_copy(x_now[:, slot, :], x_sb[:, bass.ds(j * D, D)]).then_inc(x_placed, 1)

            pool.wait_ge(x_in, 16 * 3)
            node_steps(pool, place)
            pool.wait_ge(tables_out, 32)

            outside_count = pool.alloc_register("outside_count")
            pool.reg_mov(outside_count, 0)

            def gather(q, s):
                g = 2 * q + s
                pool.wait_ge(ids_ready, g + 1)
                if past(g, 2):
                    pool.wait_ge(h_ready, g - 1)
                pool.sem_inc(gather_go, 1)
                for k in range(TILES):
                    pool.indirect_dma_start(gat[:, s, k, :], None, xa_rows,
                                            bass.IndirectOffsetOnAxis(ap=src_now[s][:, k:k + 1], axis=0)
                                            ).then_inc(gat_in[s], 16)
                outside = pool.value_load(win_i[0:1, 1, s, bass.ds(q, 1)], min_val=0, max_val=1)
                with pool.If(outside):
                    pool.wait_ge(gat_in[s], 16 * TILES * (q + 1))
                    pool.sem_inc(gather_go, 1)
                    for k in range(TILES):
                        pool.indirect_dma_start(gat[:, s, k, :], None, xb_rows,
                                                bass.IndirectOffsetOnAxis(ap=dst_now[s][:, k:k + 1], axis=0),
                                                compute_op=ALU.add).then_inc(outside_in, 16)
                    pool.reg_add(outside_count, outside_count, 16 * TILES)
                    pool.wait_ge(outside_in, pool.snap(outside_count))
                    pool.sem_inc(gather_go, 1)
                pool.sem_inc(settled, 1)

            def scatter(q, s):
                g = 2 * q + s
                pool.wait_ge(rows_ready, g + 1)
                pool.wait_ge(summed_ready, g + 1)
                for k in range(TILES):
                    if past(g, 1):
                        pool.wait_ge(acc_added[k], 16 * g)
                    pool.sem_inc(scatter_go, 1)
                    pool.indirect_dma_start(acc[k], bass.IndirectOffsetOnAxis(ap=row_now[s][:, k:k + 1], axis=0),
                                            summed[:, s, k, :], None, compute_op=ALU.add).then_inc(acc_added[k], 16)

            def step(q, s):
                nxt = after(q, s)
                if nxt:
                    gather(*nxt)
                if before(q, s):
                    scatter(*before(q, s))

            gather(0, 0)
            pool.wait_ge(acc_set, 16 * (ACCS + 1))
            run_pairs(pool, step)
            scatter(PAIRS - 1, 1)
            for c in range(CHUNKS):
                pool.wait_ge(back_in[c], 16 * ACCS)
                pool.tensor_tensor(big[:, 2, c * CH * D:(c + 1) * CH * D], big[:, 2, c * CH * D:(c + 1) * CH * D],
                                   big[:, 3, c * CH * D:(c + 1) * CH * D], ALU.add).then_inc(half_sum, 1)

        @block.vector
        def _(dve):
            count = [0]

            def link(ins):
                count[0] += 1
                ins.then_inc(dve_step, 1)
                dve.wait_ge(dve_step, count[0])

            dve.memset(ones[:], 1.0)
            dve.memset(eps[:], EPS)
            link(dve.memset(bias2[:, 1, :], 0.0))
            dve.wait_ge(small_in, 64)
            for c in range(3):
                dve.tensor_reduce(wmean[:, c:c + 1], w[:, c, :], AX.X, ALU.add)
            link(dve.tensor_reduce(wmean[:, 3:4], bias2[:, 0, :], AX.X, ALU.add))
            link(dve.tensor_scalar(wmean[:], wmean[:], 1.0 / D, None, ALU.mult))
            for c in range(3):
                dve.tensor_scalar(w[:, c, :], w[:, c, :], wmean[:, c:c + 1], None, ALU.subtract)
            link(dve.tensor_scalar(bias2[:, 0, :], bias2[:, 0, :], wmean[:, 3:4], None, ALU.subtract))
            dve.wait_ge(con_in, 16)
            link(dve.tensor_copy(ident_h[:], ident))
            dve.nop().then_inc(prep_ready, 1)

            dve.wait_ge(ids_in, 16 * 6)
            dve.tensor_copy(ids_f[:], ids_i[:])
            link(dve.tensor_scalar(low_i[:], ids_i[:], P - 1, None, ALU.bitwise_and))
            dve.tensor_copy(low_h[:], low_i[:])
            link(dve.tensor_tensor(high_h[:], ids_i[:], low_i[:], ALU.subtract))
            df = ids_f[:, 1, :].rearrange("p (s e) -> p s e", s=2)
            dve.tensor_reduce(span[:, 0, :], df, AX.X, ALU.min)
            link(dve.tensor_reduce(span[:, 1, :], df, AX.X, ALU.max))
            link(dve.tensor_scalar(span[:, 2, :], span[:, 0, :], float(WIN_MAX), None, ALU.min))
            link(dve.tensor_tensor(span[:, 3, :], span[:, 1, :], span[:, 2, :], ALU.subtract))
            link(dve.tensor_scalar(span[:, 3, :], span[:, 3, :], float(P), None, ALU.is_ge))
            link(dve.scalar_tensor_tensor(span[:, 1, :], span[:, 3, :], -4.0 * NPAD, span[:, 2, :], ALU.mult, ALU.add))
            for n, at in enumerate((1, 2, 3)):
                for s in range(2):
                    ins = dve.tensor_scalar(diag[:, n, s, :], ident, span[:, at, s:s + 1], None, ALU.mult)
            link(ins)
            dve.nop().then_inc(prep_ready, 1)
            for n in range(2):
                for s in range(2):
                    dve.wait_ge(prep_pe, 2 * n + s + 1)
                    got = pH[s][:, :, 0:PAIRS].rearrange("p k q -> p q k")
                    if n == 0:
                        dve.tensor_copy(src_f[:, :, s, :], got)
                        link(dve.tensor_copy(src_i[:, :, s, :], got))
                    else:
                        link(dve.tensor_copy(dst_i[:, :, s, :], got))
                    dve.nop().then_inc(prep_ready, 1)
            link(dve.tensor_scalar(to_dump[:], src_f[:], -1.0, con[:, C_DUMP:C_DUMP + 1], ALU.mult, ALU.add))
            dve.wait_ge(prep_pe, 5)
            spread = pM[:, 0:2, 0:PAIRS].rearrange("p s q -> p q s")
            link(dve.tensor_scalar(win_f[:], spread, con[:, C_IOTA:C_IOTA + 1], None, ALU.add))
            link(dve.tensor_copy(win_i[:, 0, :, :], pM[:, 2:4, 0:PAIRS]))
            link(dve.tensor_copy(win_i[:, 1, :, :], pT[:, 0:2, 0:PAIRS]))
            dve.nop().then_inc(windows_ready, 1)
            dve.nop().then_inc(prep_ready, 1)

            def keep(j, slot):
                dve.wait_ge(node_done, j + 1)
                dve.tensor_tensor(big[:, 1:3, bass.ds(j * D, D)], (pS, pD)[slot][:, 0:2 * D].rearrange("p (a d) -> p a d", a=2),
                                  bias2[:], ALU.add).then_inc(node_kept, 1)

            node_steps(dve, keep)

            def ids(q, s):
                g = 2 * q + s
                if past(q, 1):
                    dve.wait_ge(gat_in[s], 16 * TILES * q)
                if past(g, 2):
                    dve.wait_ge(settled, g - 1)
                dve.tensor_copy(src_now[s][:], src_i[:, bass.ds(q, 1), s, :].rearrange("p a k -> p (a k)"))
                dve.tensor_copy(dst_now[s][:], dst_i[:, bass.ds(q, 1), s, :].rearrange("p a k -> p (a k)")
                                ).then_inc(ids_ready, 1)

            def build(q, s):
                g = 2 * q + s
                dve.wait_ge(dst_spread, g + 1)
                if past(g, 2):
                    dve.wait_ge(h_ready, g - 1)
                dve.tensor_scalar(hot[:, s, :, :], pD[:].rearrange("p (j k) -> p k j", k=TILES),
                                  win_f[:, bass.ds(q, 1), s], None, ALU.is_equal).then_inc(hot_built, 1)
                dve.wait_ge(src_spread, g + 1)
                if past(g, 2):
                    dve.wait_ge(combined, g - 1)
                dve.tensor_tensor(same[:, s, :, :], pS[:].rearrange("p (j k) -> p k j", k=TILES),
                                  src_f[:, bass.ds(q, 1), s, :].rearrange("p a k -> p (a k)").unsqueeze(2)
                                  .to_broadcast([P, TILES, P]), ALU.is_equal).then_inc(same_built, 1)

            def scale(q, s):
                g = 2 * q + s
                dve.wait_ge(std_ready, g + 1)
                dve.reciprocal(rstd[:, s, :], std[:, s, :]).then_inc(rstd_ready, 1)
                dve.wait_ge(rstd_ready, g + 1)
                for k in range(TILES):
                    ins = dve.scalar_tensor_tensor(pH[s][:, k, :], pH[s][:, k, :], rstd[:, s, k:k + 1], gamma_b[:],
                                                   ALU.mult, ALU.mult)
                ins.then_inc(scaled, 1)
                dve.wait_ge(scaled, g + 1)
                dve.tensor_tensor(pH[s][:], pH[s][:], beta_b[:].unsqueeze(1).to_broadcast([P, TILES, D]), ALU.add
                                  ).then_inc(z_ready, 1)

            def rows(q, s):
                g = 2 * q + s
                dve.wait_ge(weighed, g + 1)
                dve.tensor_tensor(over[:], pW[:], con[:, C_THR:C_THR + 2].unsqueeze(1).to_broadcast([P, TILES, 2]),
                                  ALU.is_ge).then_inc(over_found, 1)
                dve.wait_ge(over_found, g + 1)
                dve.tensor_tensor(dup[:], over[:, :, 0], over[:, :, 1], ALU.max).then_inc(dup_found, 1)
                dve.wait_ge(dup_found, g + 1)
                dve.tensor_tensor(shift[:], dup[:], to_dump[:, bass.ds(q, 1), s, :].rearrange("p a k -> p (a k)"),
                                  ALU.mult).then_inc(shift_found, 1)
                dve.wait_ge(shift_found, g + 1)
                for k in range(ACCS):
                    if past(g, 2):
                        dve.wait_ge(acc_added[k], 16 * (g - 1))
                dve.tensor_tensor(row_now[s][:], shift[:], src_f[:, bass.ds(q, 1), s, :].rearrange("p a k -> p (a k)"),
                                  ALU.add).then_inc(rows_ready, 1)

            def step(q, s):
                nxt = after(q, s)
                nn = after(*nxt) if nxt else None
                if nxt:
                    build(*nxt)
                scale(q, s)
                if nn:
                    ids(*nn)
                rows(q, s)

            ids(0, 0)
            ids(0, 1)
            build(0, 0)
            run_pairs(dve, step)

            for c in range(CHUNKS):
                at = slice(c * CH * D, (c + 1) * CH * D)
                js = slice(c * CH, (c + 1) * CH)
                total = big[:, 0, at]
                total3 = total.rearrange("p (j d) -> p j d", d=D)
                dve.wait_ge(back_in[c], 16 * ACCS)
                link(dve.tensor_tensor(total, total, big[:, 1, at], ALU.add))
                dve.wait_ge(half_sum, c + 1)
                link(dve.tensor_tensor(total, total, big[:, 2, at], ALU.add))
                link(dve.tensor_reduce(mean[:, js], total3, AX.X, ALU.add))
                link(dve.tensor_scalar(mean[:, js], mean[:, js], 1.0 / D, None, ALU.mult))
                dve.tensor_tensor(total3, total3, mean[:, js].unsqueeze(2).to_broadcast([P, CH, D]), ALU.subtract
                                  ).then_inc(centred, 1)
                dve.wait_ge(fin_squares, c + 1)
                dve.tensor_reduce(var[:, js], big[:, 1, at].rearrange("p (j d) -> p j d", d=D), AX.X, ALU.add
                                  ).then_inc(fin_var, 1)
                dve.wait_ge(fin_std, c + 1)
                link(dve.reciprocal(rdev[:, js], sdev[:, js]))
                dve.tensor_tensor(total3, total3, rdev[:, js].unsqueeze(2).to_broadcast([P, CH, D]), ALU.mult
                                  ).then_inc(fin_done, 1)

        @block.scalar
        def _(act):
            def xT_copy(j, slot):
                act.wait_ge(x_turned, j + 1)
                if past(j, 2):
                    act.wait_ge(node_done, j - 1)
                act.copy(xT[:, slot, :], pH[slot][:, 0, :]).then_inc(xT_copied, 1)

            node_steps(act, xT_copy)

            def eaT_copy(q, s):
                g = 2 * q + s
                act.wait_ge(ea_turned, g + 1)
                if past(g, 2):
                    act.wait_ge(h_ready, g - 1)
                act.copy(eaT[:, s, :, :], pT[:]).then_inc(eaT_copied, 1)

            def step(q, s):
                g = 2 * q + s
                nxt = after(q, s)
                act.wait_ge(h_ready, g + 1)
                for k in range(TILES):
                    ins = act.activation(squared[:, s, k, :], pH[s][:, k, :], ACT.Square, accum_out=squares[:, s, k:k + 1])
                ins.then_inc(squares_done, 1)
                act.wait_ge(squares_done, g + 1)
                act.activation(std[:, s, :], squares[:, s, :], ACT.Sqrt, bias=eps[:], scale=1.0 / D).then_inc(std_ready, 1)
                if before(q, s):
                    keep_sums(*before(q, s))
                if nxt:
                    eaT_copy(*nxt)
                act.wait_ge(z_ready, g + 1)
                if past(g, 2):
                    act.wait_ge(combined, g - 1)
                act.activation(msg[:, s, :, :], pH[s][:], ACT.Relu).then_inc(msg_ready, 1)

            def keep_sums(q, s):
                g = 2 * q + s
                act.wait_ge(combined, g + 1)
                for k in range(ACCS):
                    if past(g, 2):
                        act.wait_ge(acc_added[k], 16 * (g - 1))
                act.copy(summed[:, s, :, :], pM[:]).then_inc(summed_ready, 1)

            eaT_copy(0, 0)
            run_pairs(act, step)
            keep_sums(PAIRS - 1, 1)
            for c in range(CHUNKS):
                at = slice(c * CH * D, (c + 1) * CH * D)
                js = slice(c * CH, (c + 1) * CH)
                act.wait_ge(centred, c + 1)
                act.activation(big[:, 1, at], big[:, 0, at], ACT.Square).then_inc(fin_squares, 1)
                act.wait_ge(fin_var, c + 1)
                act.activation(sdev[:, js], var[:, js], ACT.Sqrt, bias=eps[:], scale=1.0 / D).then_inc(fin_std, 1)

        @block.tensor
        def _(pe):
            pe.wait_ge(prep_ready, 2)
            for n in range(2):
                for s in range(2):
                    if n:
                        pe.wait_ge(prep_ready, 3 + s)
                    for k in range(TILES):
                        ids = ids_f[0:PAIRS, n, s * GROUP:(s + 1) * GROUP].rearrange("q (p k) -> q k p", k=TILES)
                        ins = pe.transpose(pH[s][:, k, 0:PAIRS], ids[:, k, :], ident[0:PAIRS, 0:PAIRS])
                    ins.then_inc(prep_pe, 1)
            for n in range(3):
                for s in range(2):
                    to = (pM[:, 2 * n + s, 0:PAIRS] if n < 2 else pT[:, s, 0:PAIRS])
                    ins = pe.matmul(to, ones[0:PAIRS, :], diag[0:PAIRS, n, s, 0:PAIRS], start=True, stop=True)
            ins.then_inc(prep_pe, 1)
            pe.wait_ge(prep_ready, 7)

            def turn_x(j, slot):
                if past(j, 2):
                    pe.wait_ge(xT_copied, j - 1)
                pe.wait_ge(x_placed, j + 1)
                pe.transpose(pH[slot][:, 0, :], x_now[:, slot, :], ident).then_inc(x_turned, 1)

            def node(j, slot):
                pe.wait_ge(xT_copied, j + 1)
                if past(j, 2):
                    pe.wait_ge(node_kept, j - 1)
                pe.matmul((pS, pD)[slot][:, 0:2 * D], xT[:, slot, :], w[:, 0:2, :].rearrange("p a d -> p (a d)"),
                          start=True, stop=True).then_inc(node_done, 1)

            def node_step(j, slot):
                if not (isinstance(j, int) and j == R - 1):
                    turn_x(j + 1, 1 - slot)
                node(j, slot)

            turn_x(0, 0)
            node_steps(pe, node_step)

            def front(q, s):
                g = 2 * q + s
                tail = isinstance(q, int) and g == 2 * PAIRS - 1 and TAIL % TILES
                if isinstance(q, int) and g == 0:
                    pe.wait_ge(xT_copied, R)
                    pe.wait_ge(node_kept, R)
                for n, to, used, ready in ((1, pD, hot_built, dst_spread), (0, pS, same_built, src_spread)):
                    if past(g, 1):
                        pe.wait_ge(used, g)
                    pick = ident_h[0:PAIRS, bass.ds(q, 1)].to_broadcast([PAIRS, P])
                    pe.matmul(to[:], pick, high_h[0:PAIRS, n, s * GROUP:(s + 1) * GROUP], start=True, stop=False)
                    pe.matmul(to[:], pick, low_h[0:PAIRS, n, s * GROUP:(s + 1) * GROUP], start=False, stop=True
                              ).then_inc(ready, 1)
                pe.wait_ge(ea_in[s], 16 * (q + 2) if tail else 16 * (q + 1))
                if past(g, 1):
                    pe.wait_ge(eaT_copied, g)
                for k in range(TILES):
                    ins = pe.transpose(pT[:, k, :], ea[:, s, k, :], ident)
                ins.then_inc(ea_turned, 1)

            def weigh(q, s):
                g = 2 * q + s
                pe.wait_ge(same_built, g + 1)
                if past(g, 1):
                    pe.wait_ge(over_found, g)
                for k in range(TILES):
                    ins = pe.matmul(pW[:, k, :], same[:, s, k, :], con[:, C_POW:C_POW + 2], start=True, stop=True)
                ins.then_inc(weighed, 1)

            def products(q, s):
                g = 2 * q + s
                pe.wait_ge(eaT_copied, g + 1)
                pe.wait_ge(hot_built, g + 1)
                pe.wait_ge(window_in[s], 16 * (q + 1))
                if past(g, 2):
                    pe.wait_ge(msg_ready, g - 1)
                pe.wait_ge(gat_in[s], 16 * TILES * (q + 1))
                pe.wait_ge(settled, g + 1)
                for k in range(TILES):
                    pe.matmul(pH[s][:, k, :], eaT[:, s, k, :], w[:, 2, :], start=True, stop=False)
                    pe.matmul(pH[s][:, k, :], hot[:, s, k, :], window[:, s, :], start=False, stop=False)
                    ins = pe.matmul(pH[s][:, k, :], ident, gat[:, s, k, :], start=False, stop=True)
                ins.then_inc(h_ready, 1)

            def combine(q, s):
                g = 2 * q + s
                pe.wait_ge(msg_ready, g + 1)
                if past(g, 1):
                    pe.wait_ge(summed_ready, g)
                for k in range(TILES):
                    ins = pe.matmul(pM[:, k, :], same[:, s, k, :], msg[:, s, k, :], start=True, stop=True)
                ins.then_inc(combined, 1)

            def step(q, s):
                nxt = after(q, s)
                products(q, s)
                if before(q, s):
                    combine(*before(q, s))
                if nxt:
                    front(*nxt)
                weigh(q, s)

            front(0, 0)
            run_pairs(pe, step)
            combine(PAIRS - 1, 1)


def kernel(x, src, dst, edge_attr_128, L0_gnn_W, L0_gnn_b, L0_gnn_gamma, L0_gnn_beta):
    import numpy as _np
    import concourse.bacc as _bacc
    from concourse import mybir as _mybir
    from concourse.bass_utils import run_bass_kernel_spmd as _run

    named = {"x": x, "src": src, "dst": dst, "edge_attr": edge_attr_128, "W": L0_gnn_W, "b": L0_gnn_b,
             "gamma": L0_gnn_gamma, "beta": L0_gnn_beta, "consts": constants(x.shape[0])}
    nc = _bacc.Bacc("TRN2", target_bir_lowering=False, num_devices=1)
    arrays, args = {}, []
    for name, a in named.items():
        a = _np.ascontiguousarray(a)
        arrays[f"in_{name}"] = a
        args.append(nc.dram_tensor(f"in_{name}", a.shape, _mybir.dt.from_np(a.dtype), kind="ExternalInput").ap())
    args.append(nc.dram_tensor("out_0", x.shape, _mybir.dt.float32, kind="ExternalOutput").ap())
    gnn_kernel(nc, *args)
    r = _run(nc, [arrays], core_ids=[0])
    return r.results[0]["out_0"]
```

```python
from contextlib import ExitStack

import concourse.bass as bass
from concourse import mybir

ALU = mybir.AluOpType
ACT = mybir.ActivationFunctionType
AX = mybir.AxisListType
F32 = mybir.dt.float32
BF16 = mybir.dt.bfloat16
I32 = mybir.dt.int32

P = 128
D = 128
TILES = 4
GROUP = TILES * P
RUN = GROUP // 2
ZW = D + 4
EPS = 1e-5

C_ID, C_ROW, C_TRI, C_IOTA, C_RUN, C_END = 0, P, 2 * P, 3 * P, 3 * P + 1, 3 * P + 5


def constants():
    import numpy as np
    c = np.zeros((P, C_END), np.float32)
    p = np.arange(P)
    c[:, C_ID:C_ID + P] = np.eye(P)
    c[:, C_ROW:C_ROW + P] = p[None, :] + 1
    c[:, C_TRI:C_TRI + P] = p[:, None] < p[None, :]
    c[:, C_IOTA] = p
    c[:, C_RUN:C_RUN + 4] = p[:, None] + P * np.arange(4)[None, :]
    return c


def gnn_kernel(nc, x, src, dst, edge, W, b, gamma, beta, consts, out):
    N, E = x.shape[0], edge.shape[0]
    BLOCKS = -(-N // P)
    LASTN = N - (BLOCKS - 1) * P
    PAIRS = -(-E // (2 * GROUP))
    NPAD = P * BLOCKS
    WIN_MAX = NPAD - P
    LASTE = E - (PAIRS - 1) * 2 * GROUP
    TAIL = LASTE - GROUP
    RUNS = (PAIRS * 2 * GROUP + BLOCKS * (RUN - 1)) // RUN
    RUNS += -RUNS % 16
    QUADS = PAIRS // 2
    OCTS = RUNS // 16
    CLEAR = RUNS
    ZROWS = (RUNS + 1 + BLOCKS) * RUN
    CH = 7
    CHUNKS = BLOCKS // CH
    assert 0 < TAIL <= GROUP and 2 < PAIRS <= P and BLOCKS == CH * CHUNKS and CHUNKS == 7 and RUNS <= 4 * P
    assert PAIRS % 2 == 0
    TN = 2 * TILES * PAIRS

    xb_rows = nc.dram_tensor("xb_rows", [NPAD, D], F32, kind="Internal").ap()
    sorted_rows = nc.dram_tensor("sorted_rows", [ZROWS, ZW], F32, kind="Internal").ap()

    with ExitStack() as ctx:
        def sb(name, shape, dt=F32):
            return ctx.enter_context(nc.sbuf_tensor(name, shape, dt))

        def ps(name, shape, dt=F32):
            return ctx.enter_context(nc.psum_tensor(name, shape, dt))

        def sem(name):
            return ctx.enter_context(nc.semaphore(name))

        con = sb("con", [P, C_END])
        w = sb("w", [P, 3, D])
        gamma_b = sb("gamma_b", [P, D])
        beta_b = sb("beta_b", [P, D])
        eps = sb("eps", [P, 1])
        total = sb("total", [P, BLOCKS, D])
        xa = sb("xa", [P, BLOCKS, D])
        sched = sb("sched", [1, 2, 4 * P], I32)
        wmean = sb("wmean", [P, 4])
        bias2 = sb("bias2", [P, 2, D])
        ones = sb("ones", [P, P])
        ones_h = sb("ones_h", [P, P], BF16)
        tri_h = sb("tri_h", [P, P], BF16)
        ident_h = sb("ident_h", [P, P], BF16)
        early = total[:].rearrange("p b d -> p (b d)")
        ids_i = early[:, 0:4 * GROUP].bitcast(I32).rearrange("p (n e) -> p n e", n=2)
        ids_f = early[:, 4 * GROUP:8 * GROUP].rearrange("p (n e) -> p n e", n=2)
        diag = early[:, 8 * GROUP:8 * GROUP + 6 * P].rearrange("p (n s k) -> p n s k", n=3, s=2)
        low_c = early[:, 8 * GROUP + 6 * P:8 * GROUP + 6 * P + TN].bitcast(I32).rearrange("p (q s k) -> p q s k", s=2, k=TILES)
        low_h = sb("low_h", [P, 2 * GROUP], BF16)
        high_h = sb("high_h", [P, 2 * GROUP], BF16)
        src_i = sb("src_i", [P, PAIRS, 2, TILES], I32)
        dst_i = sb("dst_i", [P, PAIRS, 2, TILES], I32)
        place = sb("place", [P, PAIRS, 2, TILES])
        block_h = sb("block_h", [P, TN], BF16)
        member = sb("member", [P, BLOCKS, TN], BF16)
        span = sb("span", [P, 4, 2])
        win_f = sb("win_f", [P, PAIRS, 2])
        win_i = sb("win_i", [P, 2 * PAIRS], I32)
        flags = sb("flags", [P, 2, 2 * PAIRS + 4], I32)
        count_p = sb("count_p", [P, BLOCKS])
        count_i = sb("count_i", [P, 2, BLOCKS], I32)
        runs = sb("runs", [P, BLOCKS])
        ends = sb("ends", [P, BLOCKS])
        past_end = sb("past_end", [P, 4, BLOCKS])
        run_cols = sb("run_cols", [P, 3, 4])
        fill_a = sb("fill_a", [P, BLOCKS])
        fill_b = sb("fill_b", [P, BLOCKS])
        fill_i = sb("fill_i", [P, BLOCKS], I32)
        clear = sb("clear", [P, 2 * ZW])
        work = sb("work", [P, 4 * CH * D])
        x_now = work[:, 0:2 * CH * D].rearrange("p (s j d) -> p s j d", s=2, d=D)
        xb_now = work[:, 2 * CH * D:4 * CH * D].rearrange("p (s j d) -> p s j d", s=2, d=D)
        xT = sb("xT", [P, 2, TILES, P])
        ea = work[:, 0 * GROUP:2 * GROUP].rearrange("p (s k d) -> p s k d", s=2, k=TILES)
        eaT = work[:, 2 * GROUP:4 * GROUP].rearrange("p (s k d) -> p s k d", s=2, k=TILES)
        hot = work[:, 4 * GROUP:6 * GROUP].rearrange("p (s k d) -> p s k d", s=2, k=TILES)
        window = sb("window", [P, 2, D])
        gat = sb("gat", [P, 2, TILES, D])
        zrow = sb("zrow", [P, 4, TILES, ZW])
        free_row = sb("free_row", [1, BLOCKS])
        chosen = sb("chosen", [P, TILES, BLOCKS])
        row_f = sb("row_f", [P, TILES])
        row_now = [sb(f"row_now{s}", [P, TILES], I32) for s in range(4)]
        dst_now = [sb(f"dst_now{s}", [P, TILES], I32) for s in range(2)]
        late = member[:].rearrange("p b t -> p (b t)").bitcast(F32)[:, 0:16 * GROUP].rearrange("p (s k d) -> p s k d", s=16, k=TILES)
        hotT = late[:, 0:8, :, :]
        hot2 = late[:, 8:12, :, :]
        msg = late[:, 12:16, :, :]
        squared = sb("squared", [P, 2, TILES, D], BF16)
        squares = sb("squares", [P, 4, TILES])
        std = sb("std", [P, 4, TILES])
        rstd = sb("rstd", [P, 4, TILES])
        stats = sb("stats", [P, BLOCKS, 6])
        moments = sb("moments", [P, BLOCKS, 2])
        sdev = sb("sdev", [P, BLOCKS])
        rdev = sb("rdev", [P, BLOCKS])
        offset = sb("offset", [P, BLOCKS])
        result = x_now

        pT = ps("pT", [P, TILES, P])
        pD = ps("pD", [P, GROUP])
        pH = [ps(f"pH{s}", [P, TILES, D]) for s in range(2)]
        pM = ps("pM", [P, TILES, D])
        pS = ps("pS", [P, GROUP])
        pR = ps("pR", [P, GROUP])
        pX = ps("pX", [P, TILES, P])
        next_rows = pR[:, 0:(TILES + 1) * BLOCKS].rearrange("p (k b) -> p k b", b=BLOCKS)
        by_tile = "p (k d) -> p k d"
        h_bank = [pH[0][:], pH[1][:], pS[:].rearrange(by_tile, d=D), pD[:].rearrange(by_tile, d=D)]
        turn_bank = [pT[:], pX[:]]
        sum_bank = [pM[:], pR[:].rearrange(by_tile, d=D)]

        ident = con[:, C_ID:C_ID + P]
        row_1 = con[:, C_ROW:C_ROW + P]
        iota = con[:, C_IOTA:C_IOTA + 1]

        con_in = sem("con_in")
        small_in = sem("small_in")
        x_in = [sem(f"x_in{s}") for s in range(2)]
        total_in = sem("total_in")
        ids_in = sem("ids_in")
        pads_set = sem("pads_set")
        clear_set = sem("clear_set")
        dve_step = sem("dve_step")
        weights_ready = sem("weights_ready")
        ids_split = sem("ids_split")
        cols_turned = sem("cols_turned")
        cols_read = sem("cols_read")
        spans_spread = sem("spans_spread")
        windows_ready = sem("windows_ready")
        members_ready = sem("members_ready")
        counted = sem("counted")
        runs_found = sem("runs_found")
        runs_turned = sem("runs_turned")
        fills_ready = sem("fills_ready")
        sched_ready = sem("sched_ready")
        filled = sem("filled")
        x_turned = sem("x_turned")
        xT_copied = sem("xT_copied")
        node_done = [sem(f"node_done{i}") for i in range(4)]
        node_kept = [sem(f"node_kept{i}") for i in range(4)]
        xb_out = [sem(f"xb_out{s}") for s in range(2)]
        ea_in = [sem(f"ea_in{s}") for s in range(2)]
        window_in = [sem(f"window_in{s}") for s in range(2)]
        outside_in = sem("outside_in")
        sorted_out = [sem(f"sorted_out{s}") for s in range(4)]
        pool_go = sem("pool_go")
        gather_ready = sem("gather_ready")
        settled = sem("settled")
        ea_turned = sem("ea_turned")
        eaT_copied = sem("eaT_copied")
        dst_spread = sem("dst_spread")
        hot_built = sem("hot_built")
        h_ready = sem("h_ready")
        rows_kept = sem("rows_kept")
        free_found = sem("free_found")
        free_kept = sem("free_kept")
        chosen_ready = sem("chosen_ready")
        row_found = sem("row_found")
        row_ready = sem("row_ready")
        z_in = [sem(f"z_in{s}") for s in range(4)]
        hotT_built = sem("hotT_built")
        hotT_turned = sem("hotT_turned")
        hot2_copied = sem("hot2_copied")
        xa_picked = sem("xa_picked")
        h2_ready = sem("h2_ready")
        squares_done = sem("squares_done")
        std_ready = sem("std_ready")
        rstd_ready = sem("rstd_ready")
        scaled = sem("scaled")
        shifted = sem("shifted")
        msg_ready = sem("msg_ready")
        summed = sem("summed")
        added = sem("added")
        fin_var = sem("fin_var")
        fin_std = sem("fin_std")
        fin_scale = sem("fin_scale")
        fin_done = sem("fin_done")
        stored = [sem(f"stored{s}") for s in range(2)]

        def past(at, n):
            return not isinstance(at, int) or at >= n

        def run_quads(eng, step, load=None):
            def four(q):
                if load:
                    load(q)
                for s in range(4):
                    step(q, s)

            four(0)
            with eng.Fori(1, QUADS - 1) as q:
                four(q)
            four(QUADS - 1)

        def run_octs(eng, step, load=None):
            def eight(q):
                for s in range(8):
                    if load and s % 4 == 0:
                        load(2 * q + s // 4)
                    step(q, s)

            eight(0)
            with eng.Fori(1, OCTS - 1) as q:
                eight(q)
            eight(OCTS - 1)

        def shift(q, s, n, steps, width):
            at, slot = (s + n) // width, (s + n) % width
            if isinstance(q, int):
                return (q + at, slot) if 0 <= q + at < steps else None
            return (q if at == 0 else q + at), slot

        def registers(eng, name, n):
            regs = [eng.alloc_register(f"{name}{i}") for i in range(n)]

            def load(table, at, most):
                eng.load(regs, table[0:1, bass.ds(at, n)])
                return [eng.snap(reg, min_val=0, max_val=most) for reg in regs]
            return load

        def run_chunks(eng, step):
            step(0, 0)
            step(1, 1)
            with eng.Fori(1, CHUNKS // 2) as i:
                step(2 * i, 0)
                step(2 * i + 1, 1)
            step(CHUNKS - 1, 0)

        BATCHES = ((0, TILES), (TILES, CH))
        BANKS = ((0, 2), (2, 4), (4, 6), (6, 7))
        node_bank = (pS[:], pD[:], pM[:].rearrange("p k d -> p (k d)"), pT[:].rearrange("p k j -> p (k j)"))

        def column(table, q, s):
            return table[:, bass.ds(2 * q + s // 2, 1), s % 2, :].rearrange("p a k -> p (a k)")

        def clear_runs(eng, name, first, count):
            load_fills = registers(eng, name, 4)
            with eng.Fori(0, count // 4) as i:
                for at in load_fills(fill_i, i * 4 + first, ZROWS - RUN):
                    eng.dma_start(sorted_rows[bass.ds(at, RUN), :].rearrange("(p k) d -> p (k d)", p=P), clear[:]
                                  ).then_inc(filled, 16)
            for i in range(first + count // 4 * 4, first + count):
                at = eng.value_load(fill_i[0:1, i:i + 1], min_val=0, max_val=ZROWS - RUN)
                eng.dma_start(sorted_rows[bass.ds(at, RUN), :].rearrange("(p k) d -> p (k d)", p=P), clear[:]
                              ).then_inc(filled, 16)

        FILLS_SP = BLOCKS // 8 * 4

        block = ctx.enter_context(nc.Block())

        @block.sync
        def _(sp):
            sp.dma_start(con[:], consts).then_inc(con_in, 16)
            sp.dma_start(w[:], W.rearrange("(c k) n -> k c n", k=P)).then_inc(small_in, 16)
            for row, to in ((b, bias2[:, 0, :]), (gamma, gamma_b[:]), (beta, beta_b[:])):
                sp.dma_start(to, row.rearrange("(a d) -> a d", a=1).to_broadcast([P, D])).then_inc(small_in, 16)
            sp.wait_ge(pads_set, 1)
            full = PAIRS - 1
            for n, ids in enumerate((src, dst)):
                for a, z in ((0, full // 16 * 16), (full // 16 * 16, full)):
                    sp.dma_start(ids_i[a:z, n, :], ids[a * 2 * GROUP:z * 2 * GROUP].rearrange("(p e) -> p e", e=2 * GROUP)
                                 ).then_inc(ids_in, 16)
                sp.dma_start(ids_i[full:full + 1, n, 0:LASTE],
                             ids[full * 2 * GROUP:E].rearrange("(p e) -> p e", p=1)).then_inc(ids_in, 16)
            for c in range(CHUNKS):
                slot, b0 = c % 2, c * CH
                if c >= 2:
                    sp.wait_ge(x_turned, 2 * (c - 1))
                whole = min(CH, BLOCKS - 1 - b0)
                sp.dma_start(x_now[:, slot, 0:whole, :], x[b0 * P:(b0 + whole) * P, :].rearrange("(j p) d -> p j d", p=P)
                             ).then_inc(x_in[slot], 32 if whole == CH else 16)
                if whole < CH:
                    sp.dma_start(x_now[0:LASTN, slot, whole, :], x[(b0 + whole) * P:N, :]).then_inc(x_in[slot], 16)
            sp.wait_ge(clear_set, 1)
            sp.dma_start(sorted_rows[CLEAR * RUN:(CLEAR + 1) * RUN, :].rearrange("(p k) d -> p (k d)", p=P), clear[:]
                         ).then_inc(filled, 16)
            sp.wait_ge(fills_ready, 1)
            clear_runs(sp, "sp_fill", 0, FILLS_SP)
            sp.wait_ge(xb_out[0], 16 * (CHUNKS - CHUNKS // 2))
            sp.wait_ge(xb_out[1], 16 * (CHUNKS // 2))
            sp.wait_ge(windows_ready, 1)

            def load_edges(q, s):
                g, pair, h = 4 * q + s, 2 * q + s // 2, s % 2
                if past(g, 2):
                    sp.wait_ge(ea_turned, g - 1)
                if isinstance(q, int) and g == 2 * PAIRS - 1:
                    at, pt = g * GROUP, TAIL // TILES
                    sp.dma_start(ea[0:pt, h, :, :], edge[at:at + pt * TILES, :].rearrange("(p k) d -> p k d", k=TILES)
                                 ).then_inc(ea_in[h], 16)
                    if TAIL % TILES:
                        sp.dma_start(ea[pt:pt + 1, h, 0:TAIL % TILES, :],
                                     edge[at + pt * TILES:E, :].rearrange("(p k) d -> p k d", p=1)).then_inc(ea_in[h], 16)
                else:
                    sp.dma_start(ea[:, h, :, :], edge[bass.ds(g * GROUP, GROUP), :].rearrange("(p k) d -> p k d", k=TILES)
                                 ).then_inc(ea_in[h], 16)
                if past(g, 2):
                    sp.wait_ge(h_ready, g - 1)
                sp.dma_start(window[:, h, :], xb_rows[bass.ds(starts[s], P), :]).then_inc(window_in[h], 16)

            load_starts = registers(sp, "start", 4)
            starts = []

            def starts_of(q):
                starts[:] = load_starts(win_i, 4 * q, WIN_MAX)

            run_quads(sp, load_edges, starts_of)

            sp.wait_ge(pads_set, 2)
            sp.dma_start(total[:, 0:BLOCKS - 1, :], x[0:(BLOCKS - 1) * P, :].rearrange("(j p) d -> p j d", p=P)
                         ).then_inc(total_in, 16)
            sp.dma_start(total[0:LASTN, BLOCKS - 1, :], x[(BLOCKS - 1) * P:N, :]).then_inc(total_in, 16)

            for s in range(4):
                sp.wait_ge(sorted_out[s], 16 * TILES * QUADS)

            load_firsts = registers(sp, "first", 8)
            firsts = []

            def firsts_of(n):
                firsts[:] = load_firsts(sched[:, 1, :], 8 * n, CLEAR * RUN)

            def load_sorted(q, s):
                g, r = 8 * q + s, s % 4
                if past(g, 4):
                    sp.wait_ge(h2_ready, g - 3)
                for u in range(2):
                    sp.dma_start(zrow[:, r, 2 * u:2 * u + 2, :].rearrange("p k d -> p (k d)"),
                                 sorted_rows[bass.ds(firsts[2 * r + u], RUN), :].rearrange("(p k) d -> p (k d)", p=P)
                                 ).then_inc(z_in[r], 16)

            run_octs(sp, load_sorted, firsts_of)

            for c in range(CHUNKS):
                slot, b0 = c % 2, c * CH
                whole = min(CH, BLOCKS - 1 - b0)
                sp.wait_ge(fin_done, c + 1)
                sp.dma_start(out[b0 * P:(b0 + whole) * P, :].rearrange("(j p) d -> p j d", p=P), result[:, slot, 0:whole, :]
                             ).then_inc(stored[slot], 32 if whole == CH else 16)
                if whole < CH:
                    sp.dma_start(out[(b0 + whole) * P:N, :], result[0:LASTN, slot, whole, :]).then_inc(stored[slot], 16)
            sp.wait_ge(stored[0], 32 * (CHUNKS - CHUNKS // 2))
            sp.wait_ge(stored[1], 32 * (CHUNKS // 2))

        @block.gpsimd
        def _(pool):
            pool.memset(ids_i[:, 0, :], NPAD - 1)
            pool.memset(ids_i[:, 1, :], N - 1).then_inc(pads_set, 1)
            pool.memset(clear[:], 0.0).then_inc(clear_set, 1)
            pool.memset(flags[:], 0)
            pool.memset(zrow[:], 0.0).then_inc(clear_set, 1)

            def store_xb(c, slot):
                for i in range(4):
                    pool.wait_ge(node_kept[i], c + 1)
                pool.dma_start(xb_rows[bass.ds(c * CH * P, CH * P), :].rearrange("(j p) d -> p j d", p=P),
                               xb_now[:, slot, :, :]).then_inc(xb_out[slot], 16)

            run_chunks(pool, store_xb)
            pool.wait_ge(members_ready, 1)
            pool.memset(total[:, BLOCKS - 1, :], 0.0).then_inc(pads_set, 1)
            pool.wait_ge(xb_out[0], 16 * (CHUNKS - CHUNKS // 2))
            pool.wait_ge(xb_out[1], 16 * (CHUNKS // 2))
            pool.wait_ge(windows_ready, 1)
            pool.wait_ge(filled, 16 * (BLOCKS + 1))

            outside_count = pool.alloc_register("outside_count")
            pool.reg_mov(outside_count, 0)

            load_flags = registers(pool, "outside", 4)
            outside = []

            def flags_of(q):
                outside[:] = load_flags(flags[:, 1, :], 4 * q + 4, 1)

            def gather(q, s, flag):
                g, h = 4 * q + s, s % 2
                with pool.If(flag):
                    pool.wait_ge(gather_ready, g + 1)
                    if past(g, 2):
                        pool.wait_ge(rows_kept, g - 1)
                    pool.sem_inc(pool_go, 1)
                    for k in range(TILES):
                        pool.indirect_dma_start(gat[:, h, k, :], None, xb_rows,
                                                bass.IndirectOffsetOnAxis(ap=dst_now[h][:, k:k + 1], axis=0)
                                                ).then_inc(outside_in, 16)
                    pool.reg_add(outside_count, outside_count, 16 * TILES)
                    pool.wait_ge(outside_in, pool.snap(outside_count))
                    pool.sem_inc(pool_go, 1)
                pool.sem_inc(settled, 1)

            def scatter(q, s):
                g = 4 * q + s
                pool.wait_ge(row_ready, g + 1)
                pool.wait_ge(rows_kept, g + 1)
                pool.sem_inc(pool_go, 1)
                for k in range(TILES):
                    pool.indirect_dma_start(sorted_rows, bass.IndirectOffsetOnAxis(ap=row_now[s][:, k:k + 1], axis=0),
                                            zrow[:, s, k, :], None).then_inc(sorted_out[s], 16)

            def first_step(q, s):
                nxt = shift(q, s, 1, QUADS, 4)
                if nxt:
                    gather(*nxt, outside[s])
                scatter(q, s)

            gather(0, 0, pool.value_load(flags[0:1, 0, 0:1], min_val=0, max_val=1))
            run_quads(pool, first_step, flags_of)

            def build_src(q, s):
                g, r = 8 * q + s, s % 4
                pool.wait_ge(z_in[r], 32 * (2 * q + s // 4 + 1))
                if past(g, 8):
                    pool.wait_ge(summed, g - 7)
                pool.sem_inc(pool_go, 1)
                for k in range(TILES):
                    ins = pool.tensor_scalar(hotT[:, s, k, :], row_1, zrow[:, r, k, D:D + 1], None, ALU.is_equal)
                ins.then_inc(hotT_built, 1)

            run_octs(pool, build_src)

        @block.vector
        def _(dve):
            count = [0]

            def link(ins):
                count[0] += 1
                ins.then_inc(dve_step, 1)
                dve.wait_ge(dve_step, count[0])

            dve.memset(ones[:], 1.0)
            dve.memset(ones_h[:], 1.0)
            dve.memset(eps[:], EPS)
            link(dve.memset(bias2[:, 1, :], 0.0))
            dve.wait_ge(small_in, 64)
            for c in range(3):
                dve.tensor_reduce(wmean[:, c:c + 1], w[:, c, :], AX.X, ALU.add)
            link(dve.tensor_reduce(wmean[:, 3:4], bias2[:, 0, :], AX.X, ALU.add))
            link(dve.tensor_scalar(wmean[:], wmean[:], 1.0 / D, None, ALU.mult))
            for c in range(3):
                dve.tensor_scalar(w[:, c, :], w[:, c, :], wmean[:, c:c + 1], None, ALU.subtract)
            dve.tensor_scalar(bias2[:, 0, :], bias2[:, 0, :], wmean[:, 3:4], None, ALU.subtract)
            dve.wait_ge(con_in, 16)
            dve.tensor_copy(tri_h[:], con[:, C_TRI:C_TRI + P])
            dve.tensor_copy(ident_h[:], ident).then_inc(weights_ready, 1)
            dve.wait_ge(weights_ready, 1)

            dve.wait_ge(ids_in, 16 * 6)
            link(dve.tensor_copy(ids_f, ids_i))
            link(dve.tensor_scalar(ids_i[:, 0, :], ids_i[:, 1, :], P - 1, None, ALU.bitwise_and))
            dve.tensor_copy(low_h[:], ids_i[:, 0, :])
            link(dve.tensor_tensor(high_h[:], ids_i[:, 1, :], ids_i[:, 0, :], ALU.subtract))
            df = ids_f[:, 1, :].rearrange("p (s e) -> p s e", s=2)
            dve.tensor_reduce(span[:, 0, :], df, AX.X, ALU.min)
            link(dve.tensor_reduce(span[:, 1, :], df, AX.X, ALU.max))
            link(dve.tensor_scalar(span[:, 2, :], span[:, 0, :], float(WIN_MAX), None, ALU.min))
            link(dve.tensor_tensor(span[:, 3, :], span[:, 1, :], span[:, 2, :], ALU.subtract))
            link(dve.tensor_scalar(span[:, 3, :], span[:, 3, :], float(P), None, ALU.is_ge))
            link(dve.scalar_tensor_tensor(span[:, 1, :], span[:, 3, :], -4.0 * NPAD, span[:, 2, :], ALU.mult, ALU.add))
            for n, at in enumerate((1, 2, 3)):
                for s in range(2):
                    ins = dve.tensor_scalar(diag[:, n, s, :], ident, span[:, at, s:s + 1], None, ALU.mult)
            link(ins)
            dve.nop().then_inc(ids_split, 1)
            for n, to in enumerate((src_i, dst_i)):
                for s in range(2):
                    dve.wait_ge(cols_turned, 2 * n + s + 1)
                    dve.tensor_copy(to[:, :, s, :], pH[s][:, :, 0:PAIRS].rearrange("p k q -> p q k")).then_inc(cols_read, 1)
            dve.wait_ge(cols_read, 4)
            dve.wait_ge(spans_spread, 1)
            dve.tensor_scalar(win_f[:], pM[:, 0:2, 0:PAIRS].rearrange("p s q -> p q s"), iota, None, ALU.add)
            dve.tensor_copy(win_i[:].rearrange("p (q s) -> p q s", s=2), pM[:, 2:4, 0:PAIRS].rearrange("p s q -> p q s"))
            dve.wait_ge(clear_set, 2)
            for n, skip in enumerate((0, 3)):
                ins = dve.tensor_copy(flags[:, n, skip:skip + 2 * PAIRS].rearrange("p (q s) -> p q s", s=2),
                                      pT[:, 0:2, 0:PAIRS].rearrange("p s q -> p q s"))
            link(ins)
            dve.nop().then_inc(windows_ready, 1)
            link(dve.tensor_scalar(low_c, src_i[:], P - 1, None, ALU.bitwise_and))
            dve.tensor_scalar(place[:], low_c, 1.0, None, ALU.add)
            link(dve.tensor_tensor(src_i[:], src_i[:], low_c, ALU.subtract))
            link(dve.tensor_scalar(block_h[:], src_i[:].rearrange("p q s k -> p (q s k)"), 1.0 / P, 1.0, ALU.mult, ALU.add))
            with dve.Fori(0, CHUNKS) as i:
                for j in range(CH):
                    dve.tensor_scalar(member[:, bass.ds(i * CH + j, 1), :].rearrange("p a t -> p (a t)"), block_h[:],
                                      con[:, bass.ds(i * CH + j + C_ROW, 1)], None, ALU.is_equal, ALU.add,
                                      accum_out=count_p[:, bass.ds(i * CH + j, 1)]).then_inc(members_ready, 1)

            dve.wait_ge(counted, 1)
            link(dve.tensor_scalar(count_i[:, 0, :], pR[:, 0:BLOCKS], float(RUN - 1), None, ALU.add))
            link(dve.tensor_scalar(count_i[:, 1, :], count_i[:, 0, :], RUN.bit_length() - 1, None, ALU.logical_shift_right))
            link(dve.tensor_copy(runs[:], count_i[:, 1, :]))
            link(dve.tensor_tensor_scan(ends[:], ones[:, 0:BLOCKS], runs[:], 0.0, ALU.mult, ALU.add))
            link(dve.tensor_tensor(fill_a[:], ends[:], runs[:], ALU.subtract))
            link(dve.tensor_scalar(free_row[:], fill_a[0:1, :], float(RUN), None, ALU.mult))
            link(dve.tensor_scalar(fill_a[:], ends[:], float(RUN), -float(RUN), ALU.mult, ALU.add))
            link(dve.tensor_scalar(fill_b[:], con[:, C_ROW:C_ROW + BLOCKS], float(RUN), float(CLEAR * RUN), ALU.mult, ALU.add))
            link(dve.tensor_tensor(fill_b[:], fill_b[:], fill_a[:], ALU.subtract))
            link(dve.scalar_tensor_tensor(fill_b[:], runs[:], 0.0, fill_b[:], ALU.is_equal, ALU.mult))
            dve.tensor_tensor(fill_i[:, 0:BLOCKS], fill_a[:], fill_b[:], ALU.add).then_inc(fills_ready, 1)
            for i in range(4):
                ins = dve.tensor_scalar(past_end[:, i, :], ends[:], con[:, C_RUN + i:C_RUN + i + 1], None, ALU.is_le)
            link(ins)
            link(dve.tensor_reduce(run_cols[:, 2, :], past_end[:], AX.X, ALU.add))
            link(dve.tensor_scalar(run_cols[:, 0, :], run_cols[:, 2, :], BLOCKS - 1.0, None, ALU.min))
            link(dve.tensor_scalar(run_cols[:, 2, :], run_cols[:, 2, :], float(BLOCKS), None, ALU.is_ge))
            number = con[:, C_RUN:C_RUN + 4]
            link(dve.tensor_scalar(run_cols[:, 1, :], number, -float(RUN), float(CLEAR * RUN), ALU.mult, ALU.add))
            link(dve.tensor_tensor(run_cols[:, 1, :], run_cols[:, 1, :], run_cols[:, 2, :], ALU.mult))
            dve.scalar_tensor_tensor(run_cols[:, 1, :], number, float(RUN), run_cols[:, 1, :], ALU.mult, ALU.add
                                     ).then_inc(runs_found, 1)
            dve.wait_ge(runs_turned, 1)
            dve.tensor_copy(sched[:, 0, :], pX[0:1, :, :].rearrange("a k j -> a (k j)"))
            dve.tensor_copy(sched[:, 1, :], pR[0:1, :]).then_inc(sched_ready, 1)
            dve.wait_ge(sched_ready, 1)

            def place_rows(q, s):
                g = 4 * q + s
                dve.wait_ge(free_found, g + 1)
                dve.tensor_copy(free_row[:], next_rows[0:1, TILES, :]).then_inc(free_kept, 1)
                if past(g, 1):
                    dve.wait_ge(row_found, g)
                dve.tensor_tensor(chosen[:], next_rows[:, 0:TILES, :],
                                  member[:, :, bass.ds(g * TILES, TILES)].rearrange("p b k -> p k b"),
                                  ALU.mult).then_inc(chosen_ready, 1)
                dve.wait_ge(chosen_ready, g + 1)
                if past(g, 1):
                    dve.wait_ge(row_ready, g)
                dve.tensor_reduce(row_f[:], chosen[:], AX.X, ALU.add).then_inc(row_found, 1)
                dve.wait_ge(row_found, g + 1)
                if past(q, 1):
                    dve.wait_ge(sorted_out[s], 16 * TILES * q)
                dve.tensor_copy(row_now[s][:], row_f[:]).then_inc(row_ready, 1)

            def build(q, s):
                g, pair, h = 4 * q + s, 2 * q + s // 2, s % 2
                dve.wait_ge(dst_spread, g + 1)
                if past(g, 2):
                    dve.wait_ge(h_ready, g - 1)
                dve.tensor_scalar(hot[:, h, :, :], pD[:].rearrange("p (j k) -> p k j", k=TILES),
                                  win_f[:, bass.ds(pair, 1), h], None, ALU.is_equal).then_inc(hot_built, 1)

            def ids(q, s):
                g = 4 * q + s
                if past(g, 2):
                    dve.wait_ge(settled, g - 1)
                dve.tensor_copy(dst_now[s % 2][:], column(dst_i, q, s)).then_inc(gather_ready, 1)

            load_flags = registers(dve, "apart", 4)
            outside = []

            def flags_of(q):
                outside[:] = load_flags(flags[:, 0, :], 4 * q, 1)

            def keep_rows(q, s):
                g, h = 4 * q + s, s % 2
                if past(q, 1):
                    dve.wait_ge(sorted_out[s], 16 * TILES * q)
                dve.tensor_copy(zrow[:, s, :, D:D + 1].rearrange("p k a -> p (k a)"), column(place, q, s))
                with dve.If(outside[s]):
                    dve.wait_ge(h_ready, g + 1)
                    dve.wait_ge(settled, g + 1)
                    dve.tensor_tensor(zrow[:, s, :, 0:D], pH[h][:], gat[:, h, :, :], ALU.add).then_inc(rows_kept, 1)
                with dve.Else():
                    dve.wait_ge(h_ready, g + 1)
                    dve.tensor_copy(zrow[:, s, :, 0:D], pH[h][:]).then_inc(rows_kept, 1)

            def first_step(q, s):
                nxt = shift(q, s, 1, QUADS, 4)
                if nxt:
                    build(*nxt)
                    ids(*nxt)
                keep_rows(q, s)
                if nxt:
                    place_rows(*nxt)

            for slot in range(2):
                dve.wait_ge(xb_out[slot], 16 * ((CHUNKS + 1 - slot) // 2))
            ids(0, 0)
            build(0, 0)
            place_rows(0, 0)
            run_quads(dve, first_step, flags_of)

            def join(q, s):
                g, r = 8 * q + s, s % 4
                dve.wait_ge(z_in[r], 32 * (2 * q + s // 4 + 1))
                dve.wait_ge(xa_picked, g + 1)
                dve.tensor_tensor(h_bank[r], h_bank[r], zrow[:, r, :, 0:D], ALU.add).then_inc(h2_ready, 1)

            def scale(q, s):
                g, r = 8 * q + s, s % 4
                dve.wait_ge(std_ready, g + 1)
                dve.reciprocal(rstd[:, r, :], std[:, r, :]).then_inc(rstd_ready, 1)
                dve.wait_ge(rstd_ready, g + 1)
                for k in range(TILES):
                    ins = dve.scalar_tensor_tensor(h_bank[r][:, k, :], h_bank[r][:, k, :], rstd[:, r, k:k + 1], gamma_b[:],
                                                   ALU.mult, ALU.mult)
                ins.then_inc(scaled, 1)
                dve.wait_ge(scaled, g + 1)
                dve.tensor_tensor(h_bank[r], h_bank[r], beta_b[:].unsqueeze(1).to_broadcast([P, TILES, D]), ALU.add
                                  ).then_inc(shifted, 1)

            def add_sums(q, s, at):
                g = 8 * q + s
                dve.wait_ge(summed, g + 1)
                for u in range(2):
                    rows = total[:, bass.ds(at[u], 1), :].rearrange("p a d -> p (a d)")
                    if past(g, 1) or u:
                        dve.wait_ge(added, 2 * g + u)
                    dve.tensor_tensor(rows, sum_bank[s % 2][:, u, :], rows, ALU.add).then_inc(added, 1)

            load_blocks = registers(dve, "into", 8)
            into = []

            def blocks_of(n):
                if past(n, 1):
                    into[:] = load_blocks(sched[:, 0, :], 8 * n - 8, BLOCKS - 1)

            def second_step(q, s):
                if shift(q, s, -4, OCTS, 8):
                    add_sums(*shift(q, s, -4, OCTS, 8), into[2 * (s % 4):2 * (s % 4) + 2])
                join(q, s)
                if shift(q, s, -1, OCTS, 8):
                    scale(*shift(q, s, -1, OCTS, 8))

            dve.wait_ge(total_in, 32)
            run_octs(dve, second_step, blocks_of)
            scale(OCTS - 1, 7)
            blocks_of(2 * OCTS)
            for r in range(4):
                add_sums(OCTS - 1, r + 4, into[2 * r:2 * r + 2])
            dve.wait_ge(added, RUNS)

            for c in range(CHUNKS):
                js = slice(c * CH, (c + 1) * CH)
                for j in range(c * CH, (c + 1) * CH):
                    ins = dve.bn_stats(stats[:, j, :], total[:, j, :])
                link(ins)
                for j in range(c * CH, (c + 1) * CH):
                    ins = dve.bn_aggr(moments[:, j, :], stats[:, j, :])
                ins.then_inc(fin_var, 1)
                dve.wait_ge(fin_std, c + 1)
                link(dve.reciprocal(rdev[:, js], sdev[:, js]))
                dve.scalar_tensor_tensor(offset[:, js], moments[:, js, 0], -1.0, rdev[:, js], ALU.mult, ALU.mult
                                         ).then_inc(fin_scale, 1)

        @block.scalar
        def _(act):
            def xT_copy(c, slot):
                for i, (a, z) in enumerate(BATCHES):
                    act.wait_ge(x_turned, 2 * c + i + 1)
                    act.copy(xT[:, i, 0:z - a, :], pH[i][:, 0:z - a, :]).then_inc(xT_copied, 1)

            def keep(c, slot):
                if past(c, 2):
                    act.wait_ge(xb_out[slot], 8 * (c - slot))
                for i, (a, z) in enumerate(BANKS):
                    act.wait_ge(node_done[i], c + 1)
                    got = node_bank[i][:, 0:(z - a) * 2 * D].rearrange("p (j n d) -> p j n d", n=2, d=D)
                    act.copy(xa[:, bass.ds(c * CH + a, z - a), :], got[:, :, 0, :])
                    act.copy(xb_now[:, slot, a:z, :], got[:, :, 1, :]).then_inc(node_kept[i], 1)

            def node_step(c, slot):
                xT_copy(c, slot)
                keep(c, slot)

            run_chunks(act, node_step)
            act.wait_ge(fills_ready, 1)
            clear_runs(act, "act_fill", FILLS_SP, BLOCKS - FILLS_SP)

            def eaT_copy(q, s):
                g = 4 * q + s
                act.wait_ge(ea_turned, g + 1)
                if past(g, 2):
                    act.wait_ge(h_ready, g - 1)
                act.copy(eaT[:, s % 2, :, :], pT[:]).then_inc(eaT_copied, 1)

            run_quads(act, eaT_copy)

            def hot_copy(q, s):
                g, r = 8 * q + s, s % 4
                act.wait_ge(hotT_turned, g + 1)
                if past(g, 4):
                    act.wait_ge(xa_picked, g - 3)
                act.copy(hot2[:, r, :, :], turn_bank[s % 2]).then_inc(hot2_copied, 1)

            def deviation(q, s):
                g, r = 8 * q + s, s % 4
                act.wait_ge(h2_ready, g + 1)
                for k in range(TILES):
                    ins = act.activation(squared[:, s % 2, k, :], h_bank[r][:, k, :], ACT.Square,
                                         accum_out=squares[:, r, k:k + 1])
                ins.then_inc(squares_done, 1)
                act.wait_ge(squares_done, g + 1)
                act.activation(std[:, r, :], squares[:, r, :], ACT.Sqrt, bias=eps[:], scale=1.0 / D).then_inc(std_ready, 1)

            def relu(q, s):
                g, r = 8 * q + s, s % 4
                act.wait_ge(shifted, g + 1)
                if past(g, 4):
                    act.wait_ge(summed, g - 3)
                act.activation(msg[:, r, :, :], h_bank[r], ACT.Relu).then_inc(msg_ready, 1)

            def second_step(q, s):
                if shift(q, s, 1, OCTS, 8):
                    hot_copy(*shift(q, s, 1, OCTS, 8))
                deviation(q, s)
                if shift(q, s, -1, OCTS, 8):
                    relu(*shift(q, s, -1, OCTS, 8))

            hot_copy(0, 0)
            run_octs(act, second_step)
            relu(OCTS - 1, 7)

            for c in range(CHUNKS):
                slot, js = c % 2, slice(c * CH, (c + 1) * CH)
                act.wait_ge(fin_var, c + 1)
                act.activation(sdev[:, js], moments[:, js, 1], ACT.Sqrt, bias=eps[:], scale=1.0).then_inc(fin_std, 1)
                act.wait_ge(fin_scale, c + 1)
                if c >= 2:
                    act.wait_ge(stored[slot], 32 * (c // 2))
                for j in range(c * CH, (c + 1) * CH):
                    ins = act.activation(result[:, slot, j - c * CH, :], total[:, j, :], ACT.Identity,
                                         bias=offset[:, j:j + 1], scale=rdev[:, j:j + 1])
                ins.then_inc(fin_done, 1)

        @block.tensor
        def _(pe):
            pe.wait_ge(weights_ready, 1)
            pe.wait_ge(ids_split, 1)
            for n in range(2):
                for s in range(2):
                    if n:
                        pe.wait_ge(cols_read, s + 1)
                    ids = ids_f[0:PAIRS, n, s * GROUP:(s + 1) * GROUP].rearrange("q (p k) -> q k p", k=TILES)
                    for k in range(TILES):
                        ins = pe.transpose(pH[s][:, k, 0:PAIRS], ids[:, k, :], ident[0:PAIRS, 0:PAIRS])
                    ins.then_inc(cols_turned, 1)
            for n in range(3):
                for s in range(2):
                    to = (pM[:, 2 * n + s, 0:PAIRS] if n < 2 else pT[:, s, 0:PAIRS])
                    ins = pe.matmul(to, ones[0:PAIRS, :], diag[0:PAIRS, n, s, 0:PAIRS], start=True, stop=True)
            ins.then_inc(spans_spread, 1)
            pe.wait_ge(cols_read, 4)
            pe.wait_ge(windows_ready, 1)

            def node_step(c, slot):
                pe.wait_ge(x_in[slot], 16 * (c - slot) + 32)
                for i, (a, z) in enumerate(BATCHES):
                    if past(c, 1):
                        pe.wait_ge(xT_copied, 2 * c - 1 + i)
                    for j in range(a, z):
                        ins = pe.transpose(pH[i][:, j - a, :], x_now[:, slot, j, :], ident)
                    ins.then_inc(x_turned, 1)
                for m, (a, z) in enumerate(BANKS):
                    pe.wait_ge(xT_copied, 2 * c + (1 if z <= TILES else 2))
                    if past(c, 1):
                        pe.wait_ge(node_kept[m], c)
                    for j in range(a, z):
                        i = 0 if j < TILES else 1
                        to = node_bank[m][:, (j - a) * 2 * D:(j - a + 1) * 2 * D]
                        pe.matmul(to, xT[:, i, j - BATCHES[i][0], :], w[:, 0:2, :].rearrange("p n d -> p (n d)"),
                                  start=True, stop=False)
                        ins = pe.matmul(to, ones[0:1, :], bias2[0:1, :, :].rearrange("p n d -> p (n d)"),
                                        start=False, stop=True)
                    ins.then_inc(node_done[m], 1)

            run_chunks(pe, node_step)

            pe.wait_ge(members_ready, BLOCKS)
            pe.matmul(pR[:, 0:BLOCKS], ones[:], count_p[:], start=True, stop=True).then_inc(counted, 1)
            pe.wait_ge(runs_found, 1)
            for n, to in enumerate((pX[0:1, :, :].rearrange("a k j -> a (k j)"), pR[0:1, :])):
                for i in range(4):
                    ins = pe.matmul(to[:, i * P:(i + 1) * P], run_cols[:, n, i:i + 1], ident, start=True, stop=True)
            ins.then_inc(runs_turned, 1)
            pe.wait_ge(sched_ready, 1)
            for m in range(4):
                pe.wait_ge(node_kept[m], CHUNKS)

            def front(q, s):
                g, pair, h = 4 * q + s, 2 * q + s // 2, s % 2
                tail = isinstance(q, int) and g == 2 * PAIRS - 1 and TAIL % TILES
                if past(g, 1):
                    pe.wait_ge(hot_built, g)
                pick = ident_h[0:PAIRS, bass.ds(pair, 1)].to_broadcast([PAIRS, P])
                pe.matmul(pD[:], pick, high_h[0:PAIRS, h * GROUP:(h + 1) * GROUP], start=True, stop=False)
                pe.matmul(pD[:], pick, low_h[0:PAIRS, h * GROUP:(h + 1) * GROUP], start=False, stop=True
                          ).then_inc(dst_spread, 1)
                pe.wait_ge(ea_in[h], 16 * (pair + 2) if tail else 16 * (pair + 1))
                if past(g, 1):
                    pe.wait_ge(eaT_copied, g)
                for k in range(TILES):
                    ins = pe.transpose(pT[:, k, :], ea[:, h, k, :], ident)
                ins.then_inc(ea_turned, 1)

            def free_rows(q, s):
                g = 4 * q + s
                if past(g, 1):
                    pe.wait_ge(free_kept, g)
                    pe.wait_ge(chosen_ready, g)
                pe.matmul(next_rows, ones[0:1, :], free_row[:].unsqueeze(1).to_broadcast([1, TILES + 1, BLOCKS]),
                          start=True, stop=False, skip_group_check=True)
                for k in range(TILES):
                    mine = member[:, :, bass.ds(g * TILES + k, 1)].rearrange("p b a -> p a b")
                    pe.matmul(next_rows[:, k:k + 1, :], tri_h[:], mine, start=False, stop=False, skip_group_check=True)
                    ins = pe.matmul(next_rows[:, k + 1:TILES + 1, :], ones_h[:], mine.to_broadcast([P, TILES - k, BLOCKS]),
                                    start=False, stop=(k == TILES - 1), skip_group_check=True)
                ins.then_inc(free_found, 1)

            def products(q, s):
                g, pair, h = 4 * q + s, 2 * q + s // 2, s % 2
                pe.wait_ge(eaT_copied, g + 1)
                pe.wait_ge(hot_built, g + 1)
                pe.wait_ge(window_in[h], 16 * (pair + 1))
                if past(g, 2):
                    pe.wait_ge(rows_kept, g - 1)
                for k in range(TILES):
                    pe.matmul(pH[h][:, k, :], eaT[:, h, k, :], w[:, 2, :], start=True, stop=False)
                    ins = pe.matmul(pH[h][:, k, :], hot[:, h, k, :], window[:, h, :], start=False, stop=True)
                ins.then_inc(h_ready, 1)

            def first_step(q, s):
                nxt = shift(q, s, 1, QUADS, 4)
                products(q, s)
                if nxt:
                    front(*nxt)
                    free_rows(*nxt)

            front(0, 0)
            free_rows(0, 0)
            run_quads(pe, first_step)

            def turn_hot(q, s):
                g = 8 * q + s
                pe.wait_ge(hotT_built, g + 1)
                if past(g, 2):
                    pe.wait_ge(hot2_copied, g - 1)
                for k in range(TILES):
                    ins = pe.transpose(turn_bank[s % 2][:, k, :], hotT[:, s, k, :], ident)
                ins.then_inc(hotT_turned, 1)

            def pick_xa(q, s, at):
                g, r = 8 * q + s, s % 4
                pe.wait_ge(hot2_copied, g + 1)
                if past(g, 4):
                    pe.wait_ge(msg_ready, g - 3)
                for u in range(2):
                    for k in (2 * u, 2 * u + 1):
                        ins = pe.matmul(h_bank[r][:, k, :], hot2[:, r, k, :],
                                        xa[:, bass.ds(at[u], 1), :].rearrange("p a d -> p (a d)"), start=True, stop=True)
                ins.then_inc(xa_picked, 1)

            def sum_up(q, s):
                g, r = 8 * q + s, s % 4
                pe.wait_ge(msg_ready, g + 1)
                if past(g, 2):
                    pe.wait_ge(added, 2 * g - 2)
                for u in range(2):
                    for k in (2 * u, 2 * u + 1):
                        ins = pe.matmul(sum_bank[s % 2][:, u, :], hotT[:, s, k, :], msg[:, r, k, :], start=(k == 2 * u),
                                        stop=(k == 2 * u + 1))
                ins.then_inc(summed, 1)

            load_blocks = registers(pe, "of", 8)
            of = []

            def blocks_of(n):
                of[:] = load_blocks(sched[:, 0, :], 8 * n, BLOCKS - 1)

            def second_step(q, s):
                pick_xa(q, s, of[2 * (s % 4):2 * (s % 4) + 2])
                if shift(q, s, 1, OCTS, 8):
                    turn_hot(*shift(q, s, 1, OCTS, 8))
                if shift(q, s, -2, OCTS, 8):
                    sum_up(*shift(q, s, -2, OCTS, 8))

            pe.wait_ge(rows_kept, 2 * PAIRS)
            turn_hot(0, 0)
            run_octs(pe, second_step, blocks_of)
            for s in (6, 7):
                sum_up(OCTS - 1, s)


def kernel(x, src, dst, edge_attr_128, L0_gnn_W, L0_gnn_b, L0_gnn_gamma, L0_gnn_beta):
    import numpy as _np
    import concourse.bacc as _bacc
    from concourse import mybir as _mybir
    from concourse.bass_utils import run_bass_kernel_spmd as _run

    named = {"x": x, "src": src, "dst": dst, "edge_attr": edge_attr_128, "W": L0_gnn_W, "b": L0_gnn_b,
             "gamma": L0_gnn_gamma, "beta": L0_gnn_beta, "consts": constants()}
    nc = _bacc.Bacc("TRN2", target_bir_lowering=False, num_devices=1)
    arrays, args = {}, []
    for name, a in named.items():
        a = _np.ascontiguousarray(a)
        arrays[f"in_{name}"] = a
        args.append(nc.dram_tensor(f"in_{name}", a.shape, _mybir.dt.from_np(a.dtype), kind="ExternalInput").ap())
    args.append(nc.dram_tensor("out_0", x.shape, _mybir.dt.float32, kind="ExternalOutput").ap())
    gnn_kernel(nc, *args)
    r = _run(nc, [arrays], core_ids=[0])
    return r.results[0]["out_0"]
```

```python
from contextlib import ExitStack

import concourse.bass as bass
from concourse import mybir

ALU = mybir.AluOpType
ACT = mybir.ActivationFunctionType
AX = mybir.AxisListType
F32 = mybir.dt.float32
BF16 = mybir.dt.bfloat16
I32 = mybir.dt.int32

P = 128
D = 128
TILES = 4
GROUP = TILES * P
JOINED = 2
RUN = GROUP // 2
ZW = D + 4
EPS = 1e-5

C_ID, C_ROW, C_TRI, C_IOTA, C_RUN, C_END = 0, P, 2 * P, 3 * P, 3 * P + 1, 3 * P + 5


def constants():
    import numpy as np
    c = np.zeros((P, C_END), np.float32)
    p = np.arange(P)
    c[:, C_ID:C_ID + P] = np.eye(P)
    c[:, C_ROW:C_ROW + P] = p[None, :] + 1
    c[:, C_TRI:C_TRI + P] = p[:, None] < p[None, :]
    c[:, C_IOTA] = p
    c[:, C_RUN:C_RUN + 4] = p[:, None] + P * np.arange(4)[None, :]
    return c


def gnn_kernel(nc, x, src, dst, edge, W, b, gamma, beta, consts, out):
    N, E = x.shape[0], edge.shape[0]
    BLOCKS = -(-N // P)
    LASTN = N - (BLOCKS - 1) * P
    PAIRS = -(-E // (2 * GROUP))
    NPAD = P * BLOCKS
    WIN_MAX = NPAD - P
    LASTE = E - (PAIRS - 1) * 2 * GROUP
    TAIL = LASTE - GROUP
    RUNS = (PAIRS * 2 * GROUP + BLOCKS * (RUN - 1)) // RUN
    RUNS += -RUNS % 16
    QUADS = PAIRS // 2
    OCTS = RUNS // 16
    CLEAR = RUNS
    ZROWS = (RUNS + 1 + BLOCKS) * RUN
    CH = 7
    FIN_ACT = 4
    CHUNKS = BLOCKS // CH
    assert 0 < TAIL <= GROUP and 2 < PAIRS <= P and BLOCKS == CH * CHUNKS and CHUNKS == 7 and RUNS <= 4 * P
    assert PAIRS % 2 == 0
    TN = 2 * TILES * PAIRS

    xb_rows = nc.dram_tensor("xb_rows", [NPAD, D], F32, kind="Internal").ap()
    sorted_rows = nc.dram_tensor("sorted_rows", [ZROWS, ZW], F32, kind="Internal").ap()

    with ExitStack() as ctx:
        def sb(name, shape, dt=F32):
            return ctx.enter_context(nc.sbuf_tensor(name, shape, dt))

        def ps(name, shape, dt=F32):
            return ctx.enter_context(nc.psum_tensor(name, shape, dt))

        def sem(name):
            return ctx.enter_context(nc.semaphore(name))

        con = sb("con", [P, C_END])
        w = sb("w", [P, 3, D])
        gamma_b = sb("gamma_b", [P, D])
        beta_b = sb("beta_b", [P, D])
        eps = sb("eps", [P, 1])
        total = sb("total", [P, BLOCKS, D])
        xa = sb("xa", [P, BLOCKS, D])
        sched = sb("sched", [1, 2, 4 * P + 16], I32)
        wmean = sb("wmean", [P, 4])
        bias = sb("bias", [P, D])
        ones = sb("ones", [P, P])
        ones_h = sb("ones_h", [P, P], BF16)
        tri_h = sb("tri_h", [P, P], BF16)
        ident_h = sb("ident_h", [P, P], BF16)
        early = total[:].rearrange("p b d -> p (b d)")
        ids_i = early[:, 0:4 * GROUP].bitcast(I32).rearrange("p (n e) -> p n e", n=2)
        ids_f = early[:, 4 * GROUP:8 * GROUP].rearrange("p (n e) -> p n e", n=2)
        diag = early[:, 8 * GROUP:8 * GROUP + 6 * P].rearrange("p (n s k) -> p n s k", n=3, s=2)
        low_c = early[:, 8 * GROUP + 6 * P:8 * GROUP + 6 * P + TN].bitcast(I32).rearrange("p (q s k) -> p q s k", s=2, k=TILES)
        low_h = sb("low_h", [P, 2 * GROUP], BF16)
        high_h = sb("high_h", [P, 2 * GROUP], BF16)
        src_i = sb("src_i", [P, PAIRS, 2, TILES], I32)
        dst_i = sb("dst_i", [P, PAIRS, 2, TILES], I32)
        place = sb("place", [P, PAIRS, 2, TILES])
        block_h = sb("block_h", [P, TN], BF16)
        member = sb("member", [P, BLOCKS, TN], BF16)
        span = sb("span", [P, 4, 2])
        win_f = sb("win_f", [P, PAIRS, 2])
        win_i = sb("win_i", [P, 2 * PAIRS], I32)
        flags = sb("flags", [P, 2, 2 * PAIRS + 4], I32)
        count_p = sb("count_p", [P, BLOCKS])
        count_i = sb("count_i", [P, 2, BLOCKS], I32)
        runs = sb("runs", [P, BLOCKS])
        ends = sb("ends", [P, BLOCKS])
        past_end = sb("past_end", [P, 4, BLOCKS])
        run_cols = sb("run_cols", [P, 3, 4])
        fill_a = sb("fill_a", [P, BLOCKS])
        fill_b = sb("fill_b", [P, BLOCKS])
        fill_i = sb("fill_i", [P, BLOCKS], I32)
        clear = sb("clear", [P, 2 * ZW])
        work = sb("work", [P, 4 * CH * D])
        x_now = work[:, 0:2 * CH * D].rearrange("p (s j d) -> p s j d", s=2, d=D)
        xb_now = work[:, 2 * CH * D:4 * CH * D].rearrange("p (s j d) -> p s j d", s=2, d=D)
        xT = sb("xT", [P, 2, TILES, P])
        ea = work[:, 0 * GROUP:2 * GROUP].rearrange("p (s k d) -> p s k d", s=2, k=TILES)
        eaT = work[:, 2 * GROUP:4 * GROUP].rearrange("p (s k d) -> p s k d", s=2, k=TILES)
        hot = work[:, 4 * GROUP:6 * GROUP].rearrange("p (s k d) -> p s k d", s=2, k=TILES)
        window = sb("window", [P, 2, D])
        gat = sb("gat", [P, 2, TILES, D])
        zrow = sb("zrow", [P, 4, TILES, ZW])
        free_row = sb("free_row", [1, BLOCKS])
        chosen = sb("chosen", [P, TILES, BLOCKS])
        row_f = sb("row_f", [P, TILES])
        row_now = [sb(f"row_now{s}", [P, TILES], I32) for s in range(4)]
        dst_now = [sb(f"dst_now{s}", [P, TILES], I32) for s in range(2)]
        late = member[:].rearrange("p b t -> p (b t)").bitcast(F32)[:, 0:16 * GROUP].rearrange("p (s k d) -> p s k d", s=16, k=TILES)
        hotT = late[:, 0:8, :, :]
        hotT_h = member[:].rearrange("p b t -> p (b t)")[:, 0:16 * GROUP].rearrange("p (s k d h) -> p s k d h", s=8, k=TILES, h=2)
        hot2 = late[:, 8:12, :, :]
        msg = late[:, 12:16, :, :]
        squared = sb("squared", [P, 2, TILES, D], BF16)
        squares = sb("squares", [P, 4, TILES])
        std = sb("std", [P, 4, TILES])
        rstd = sb("rstd", [P, 4, TILES])
        stats = sb("stats", [P, BLOCKS, 6])
        moments = sb("moments", [P, BLOCKS, 2])
        sdev = sb("sdev", [P, BLOCKS])
        rdev = sb("rdev", [P, BLOCKS])
        offset = sb("offset", [P, BLOCKS])
        result = x_now

        pT = ps("pT", [P, TILES, P])
        pD = ps("pD", [P, GROUP])
        pH = [ps(f"pH{s}", [P, TILES, D]) for s in range(2)]
        pM = ps("pM", [P, TILES, D])
        pS = ps("pS", [P, GROUP])
        pR = ps("pR", [P, GROUP])
        pX = ps("pX", [P, TILES, P])
        next_rows = pR[:, 0:(TILES + 1) * BLOCKS].rearrange("p (k b) -> p k b", b=BLOCKS)
        by_tile = "p (k d) -> p k d"
        h_bank = [pH[0][:], pH[1][:], pS[:].rearrange(by_tile, d=D), pD[:].rearrange(by_tile, d=D)]
        turn_bank = [pT[:], pX[:]]
        sum_bank = [pM[:], pR[:].rearrange(by_tile, d=D)]

        ident = con[:, C_ID:C_ID + P]
        row_1 = con[:, C_ROW:C_ROW + P]
        iota = con[:, C_IOTA:C_IOTA + 1]

        con_in = sem("con_in")
        small_in = sem("small_in")
        x_in = [sem(f"x_in{s}") for s in range(2)]
        total_in = sem("total_in")
        ids_in = sem("ids_in")
        pads_set = sem("pads_set")
        clear_set = sem("clear_set")
        dve_step = sem("dve_step")
        weights_ready = sem("weights_ready")
        ids_split = sem("ids_split")
        cols_turned = sem("cols_turned")
        cols_read = sem("cols_read")
        spans_spread = sem("spans_spread")
        windows_ready = sem("windows_ready")
        members_ready = sem("members_ready")
        counted = sem("counted")
        runs_found = sem("runs_found")
        runs_turned = sem("runs_turned")
        fills_ready = sem("fills_ready")
        sched_ready = sem("sched_ready")
        filled = sem("filled")
        filled_rest = sem("filled_rest")
        x_turned = sem("x_turned")
        xT_copied = sem("xT_copied")
        node_done = [sem(f"node_done{i}") for i in range(4)]
        node_kept = [sem(f"node_kept{i}") for i in range(4)]
        biased = sem("biased")
        xb_out = [sem(f"xb_out{s}") for s in range(2)]
        ea_in = [sem(f"ea_in{s}") for s in range(2)]
        window_in = [sem(f"window_in{s}") for s in range(2)]
        outside_in = sem("outside_in")
        sorted_out = [sem(f"sorted_out{s}") for s in range(4)]
        pool_go = sem("pool_go")
        gather_ready = sem("gather_ready")
        settled = sem("settled")
        ea_turned = sem("ea_turned")
        eaT_copied = sem("eaT_copied")
        dst_spread = sem("dst_spread")
        hot_built = sem("hot_built")
        h_ready = sem("h_ready")
        rows_kept = sem("rows_kept")
        free_found = sem("free_found")
        free_kept = sem("free_kept")
        chosen_ready = sem("chosen_ready")
        row_found = sem("row_found")
        row_ready = sem("row_ready")
        z_in = [sem(f"z_in{s}") for s in range(4)]
        hotT_built = sem("hotT_built")
        hotT_turned = sem("hotT_turned")
        hot2_copied = sem("hot2_copied")
        xa_picked = sem("xa_picked")
        h2_ready = sem("h2_ready")
        squares_done = sem("squares_done")
        std_ready = sem("std_ready")
        rstd_ready = sem("rstd_ready")
        scaled = sem("scaled")
        shifted = sem("shifted")
        msg_ready = sem("msg_ready")
        summed = sem("summed")
        added = sem("added")
        fin_var = sem("fin_var")
        fin_std = sem("fin_std")
        fin_scale = sem("fin_scale")
        fin_done = sem("fin_done")
        fin_rest_done = sem("fin_rest_done")
        stored = [sem(f"stored{s}") for s in range(2)]

        def past(at, n):
            return not isinstance(at, int) or at >= n

        def run_quads(eng, step, load=None):
            def four(q):
                if load:
                    load(q)
                for s in range(4):
                    step(q, s)

            four(0)
            with eng.Fori(1, QUADS - 1) as q:
                four(q)
            four(QUADS - 1)

        def run_octs(eng, step, load=None):
            def eight(q):
                for s in range(8):
                    if load and s % 4 == 0:
                        load(2 * q + s // 4)
                    step(q, s)

            eight(0)
            with eng.Fori(1, OCTS - 1) as q:
                eight(q)
            eight(OCTS - 1)

        def shift(q, s, n, steps, width):
            at, slot = (s + n) // width, (s + n) % width
            if isinstance(q, int):
                return (q + at, slot) if 0 <= q + at < steps else None
            return (q if at == 0 else q + at), slot

        def registers(eng, name, n):
            regs = [eng.alloc_register(f"{name}{i}") for i in range(n)]

            def load(table, at, most):
                eng.load(regs, table[0:1, bass.ds(at, n)])
                return [eng.snap(reg, min_val=0, max_val=most) for reg in regs]
            return load

        def run_chunks(eng, step):
            step(0, 0)
            step(1, 1)
            with eng.Fori(1, CHUNKS // 2) as i:
                step(2 * i, 0)
                step(2 * i + 1, 1)
            step(CHUNKS - 1, 0)

        BATCHES = ((0, TILES), (TILES, CH))
        BANKS = ((0, 2), (2, 4), (4, 6), (6, 7))
        node_bank = (pS[:], pD[:], pM[:].rearrange("p k d -> p (k d)"), pT[:].rearrange("p k j -> p (k j)"))

        def column(table, q, s):
            return table[:, bass.ds(2 * q + s // 2, 1), s % 2, :].rearrange("p a k -> p (a k)")

        def clear_runs(eng, name, first, count, signal):
            load_fills = registers(eng, name, 4)
            with eng.Fori(0, count // 4) as i:
                for at in load_fills(fill_i, i * 4 + first, ZROWS - RUN):
                    eng.dma_start(sorted_rows[bass.ds(at, RUN), :].rearrange("(p k) d -> p (k d)", p=P), clear[:]
                                  ).then_inc(signal, 16)
            for i in range(first + count // 4 * 4, first + count):
                at = eng.value_load(fill_i[0:1, i:i + 1], min_val=0, max_val=ZROWS - RUN)
                eng.dma_start(sorted_rows[bass.ds(at, RUN), :].rearrange("(p k) d -> p (k d)", p=P), clear[:]
                              ).then_inc(signal, 16)

        FILLS_SP, FILLS_ACT = BLOCKS // 8 * 4, BLOCKS // 12 * 4

        block = ctx.enter_context(nc.Block())

        @block.sync
        def _(sp):
            sp.dma_start(con[:], consts).then_inc(con_in, 16)
            sp.dma_start(w[:], W.rearrange("(c k) n -> k c n", k=P)).then_inc(small_in, 16)
            for row, to in ((b, bias[:]), (gamma, gamma_b[:]), (beta, beta_b[:])):
                sp.dma_start(to, row.rearrange("(a d) -> a d", a=1).to_broadcast([P, D])).then_inc(small_in, 16)
            def load_x(c):
                slot, b0 = c % 2, c * CH
                if c >= 2:
                    sp.wait_ge(x_turned, 2 * (c - 1))
                whole = min(CH, BLOCKS - 1 - b0)
                sp.dma_start(x_now[:, slot, 0:whole, :], x[b0 * P:(b0 + whole) * P, :].rearrange("(j p) d -> p j d", p=P)
                             ).then_inc(x_in[slot], 32 if whole == CH else 16)
                if whole < CH:
                    sp.dma_start(x_now[0:LASTN, slot, whole, :], x[(b0 + whole) * P:N, :]).then_inc(x_in[slot], 16)

            load_x(0)
            sp.wait_ge(pads_set, 1)
            full = PAIRS - 1
            for n, ids in enumerate((src, dst)):
                for a, z in ((0, full // 16 * 16), (full // 16 * 16, full)):
                    sp.dma_start(ids_i[a:z, n, :], ids[a * 2 * GROUP:z * 2 * GROUP].rearrange("(p e) -> p e", e=2 * GROUP)
                                 ).then_inc(ids_in, 16)
                sp.dma_start(ids_i[full:full + 1, n, 0:LASTE],
                             ids[full * 2 * GROUP:E].rearrange("(p e) -> p e", p=1)).then_inc(ids_in, 16)
            for c in range(1, CHUNKS):
                load_x(c)
            sp.wait_ge(clear_set, 1)
            sp.dma_start(sorted_rows[CLEAR * RUN:(CLEAR + 1) * RUN, :].rearrange("(p k) d -> p (k d)", p=P), clear[:]
                         ).then_inc(filled, 16)
            sp.wait_ge(fills_ready, 1)
            clear_runs(sp, "sp_fill", 0, FILLS_SP, filled)
            sp.wait_ge(xb_out[0], 16 * (CHUNKS - CHUNKS // 2))
            sp.wait_ge(xb_out[1], 16 * (CHUNKS // 2))
            sp.wait_ge(windows_ready, 1)

            def load_edges(q, s):
                g, pair, h = 4 * q + s, 2 * q + s // 2, s % 2
                if past(g, 2):
                    sp.wait_ge(ea_turned, g - 1)
                if isinstance(q, int) and g == 2 * PAIRS - 1:
                    at, pt = g * GROUP, TAIL // TILES
                    sp.dma_start(ea[0:pt, h, :, :], edge[at:at + pt * TILES, :].rearrange("(p k) d -> p k d", k=TILES)
                                 ).then_inc(ea_in[h], 16)
                    if TAIL % TILES:
                        sp.dma_start(ea[pt:pt + 1, h, 0:TAIL % TILES, :],
                                     edge[at + pt * TILES:E, :].rearrange("(p k) d -> p k d", p=1)).then_inc(ea_in[h], 16)
                else:
                    sp.dma_start(ea[:, h, :, :], edge[bass.ds(g * GROUP, GROUP), :].rearrange("(p k) d -> p k d", k=TILES)
                                 ).then_inc(ea_in[h], 16)
                if past(g, 2):
                    sp.wait_ge(h_ready, g - 1)
                sp.dma_start(window[:, h, :], xb_rows[bass.ds(starts[s], P), :]).then_inc(window_in[h], 16)

            load_starts = registers(sp, "start", 4)
            starts = []

            def starts_of(q):
                starts[:] = load_starts(win_i, 4 * q, WIN_MAX)

            run_quads(sp, load_edges, starts_of)

            sp.wait_ge(pads_set, 2)
            sp.dma_start(total[:, 0:BLOCKS - 1, :], x[0:(BLOCKS - 1) * P, :].rearrange("(j p) d -> p j d", p=P)
                         ).then_inc(total_in, 16)
            sp.dma_start(total[0:LASTN, BLOCKS - 1, :], x[(BLOCKS - 1) * P:N, :]).then_inc(total_in, 16)

            for s in range(4):
                sp.wait_ge(sorted_out[s], 16 * TILES * QUADS)

            load_firsts = registers(sp, "first", 8)
            firsts = []

            def firsts_of(n):
                firsts[:] = load_firsts(sched[:, 1, :], 8 * n + 8, CLEAR * RUN)

            def load_sorted(q, s):
                g, r = 8 * q + s, s % 4
                if past(g, 4):
                    sp.wait_ge(h2_ready, g - 3)
                for u in range(2):
                    sp.dma_start(zrow[:, r, 2 * u:2 * u + 2, :].rearrange("p k d -> p (k d)"),
                                 sorted_rows[bass.ds(firsts[2 * r + u], RUN), :].rearrange("(p k) d -> p (k d)", p=P)
                                 ).then_inc(z_in[r], 16)

            run_octs(sp, load_sorted, firsts_of)

            for c in range(CHUNKS):
                slot, b0 = c % 2, c * CH
                whole = min(CH, BLOCKS - 1 - b0)
                sp.wait_ge(fin_done, c + 1)
                sp.wait_ge(fin_rest_done, c + 1)
                sp.dma_start(out[b0 * P:(b0 + whole) * P, :].rearrange("(j p) d -> p j d", p=P), result[:, slot, 0:whole, :]
                             ).then_inc(stored[slot], 32 if whole == CH else 16)
                if whole < CH:
                    sp.dma_start(out[(b0 + whole) * P:N, :], result[0:LASTN, slot, whole, :]).then_inc(stored[slot], 16)
            sp.wait_ge(stored[0], 32 * (CHUNKS - CHUNKS // 2))
            sp.wait_ge(stored[1], 32 * (CHUNKS // 2))

        @block.gpsimd
        def _(pool):
            pool.memset(ids_i[:, 0, :], NPAD - 1)
            pool.memset(ids_i[:, 1, :], N - 1).then_inc(pads_set, 1)
            pool.memset(clear[:], 0.0).then_inc(clear_set, 1)
            pool.memset(flags[:], 0)
            pool.memset(zrow[:], 0.0).then_inc(clear_set, 1)

            def store_xb(c, slot):
                for i in range(4):
                    pool.wait_ge(node_kept[i], c + 1)
                pool.dma_start(xb_rows[bass.ds(c * CH * P, CH * P), :].rearrange("(j p) d -> p j d", p=P),
                               xb_now[:, slot, :, :]).then_inc(xb_out[slot], 16)
                rows = xa[:, bass.ds(c * CH, CH), :]
                pool.tensor_tensor(rows, rows, bias[:].unsqueeze(1).to_broadcast([P, CH, D]), ALU.add).then_inc(biased, 1)

            run_chunks(pool, store_xb)
            pool.wait_ge(members_ready, 1)
            pool.memset(total[:, BLOCKS - 1, :], 0.0).then_inc(pads_set, 1)
            pool.wait_ge(xb_out[0], 16 * (CHUNKS - CHUNKS // 2))
            pool.wait_ge(xb_out[1], 16 * (CHUNKS // 2))
            pool.wait_ge(windows_ready, 1)
            pool.wait_ge(fills_ready, 1)
            clear_runs(pool, "pool_fill", FILLS_SP + FILLS_ACT, BLOCKS - FILLS_SP - FILLS_ACT, filled_rest)
            pool.wait_ge(filled, 16 * (FILLS_SP + FILLS_ACT + 1))
            pool.wait_ge(filled_rest, 16 * (BLOCKS - FILLS_SP - FILLS_ACT))

            outside_count = pool.alloc_register("outside_count")
            pool.reg_mov(outside_count, 0)

            load_flags = registers(pool, "outside", 4)
            outside = []

            def flags_of(q):
                outside[:] = load_flags(flags[:, 1, :], 4 * q + 4, 1)

            def gather(q, s, flag):
                g, h = 4 * q + s, s % 2
                with pool.If(flag):
                    pool.wait_ge(gather_ready, g + 1)
                    if past(g, 2):
                        pool.wait_ge(rows_kept, g - 1)
                    pool.sem_inc(pool_go, 1)
                    for k in range(TILES):
                        pool.indirect_dma_start(gat[:, h, k, :], None, xb_rows,
                                                bass.IndirectOffsetOnAxis(ap=dst_now[h][:, k:k + 1], axis=0)
                                                ).then_inc(outside_in, 16)
                    pool.reg_add(outside_count, outside_count, 16 * TILES)
                    pool.wait_ge(outside_in, pool.snap(outside_count))
                    pool.sem_inc(pool_go, 1)
                pool.sem_inc(settled, 1)

            def scatter(q, s):
                g = 4 * q + s
                pool.wait_ge(row_ready, g + 1)
                pool.wait_ge(rows_kept, g + 1)
                pool.sem_inc(pool_go, 1)
                for k in range(TILES):
                    pool.indirect_dma_start(sorted_rows, bass.IndirectOffsetOnAxis(ap=row_now[s][:, k:k + 1], axis=0),
                                            zrow[:, s, k, :], None).then_inc(sorted_out[s], 16)

            def first_step(q, s):
                nxt = shift(q, s, 1, QUADS, 4)
                if nxt:
                    gather(*nxt, outside[s])
                scatter(q, s)

            gather(0, 0, pool.value_load(flags[0:1, 0, 0:1], min_val=0, max_val=1))
            run_quads(pool, first_step, flags_of)

            def build_src(q, s):
                g, r = 8 * q + s, s % 4
                pool.wait_ge(z_in[r], 32 * (2 * q + s // 4 + 1))
                if past(g, 8):
                    pool.wait_ge(summed, g - 7)
                pool.sem_inc(pool_go, 1)
                for k in range(TILES):
                    ins = pool.tensor_scalar(hotT[:, s, k, :], row_1, zrow[:, r, k, D:D + 1], None, ALU.is_equal)
                ins.then_inc(hotT_built, 1)

            run_octs(pool, build_src)

            for c in range(CHUNKS):
                slot = c % 2
                pool.wait_ge(fin_scale, c + 1)
                if c >= 2:
                    pool.wait_ge(stored[slot], 32 * (c // 2))
                for j in range(FIN_ACT, CH):
                    at = c * CH + j
                    ins = pool.tensor_scalar(result[:, slot, j, :], total[:, at, :], rdev[:, at:at + 1], offset[:, at:at + 1],
                                             ALU.mult, ALU.add)
                ins.then_inc(fin_rest_done, 1)

        @block.vector
        def _(dve):
            count = [0]

            def link(ins):
                count[0] += 1
                ins.then_inc(dve_step, 1)
                dve.wait_ge(dve_step, count[0])

            dve.memset(ones[:], 1.0)
            dve.memset(ones_h[:], 1.0)
            dve.memset(eps[:], EPS)
            dve.wait_ge(small_in, 64)
            for c in range(3):
                dve.tensor_reduce(wmean[:, c:c + 1], w[:, c, :], AX.X, ALU.add)
            link(dve.tensor_reduce(wmean[:, 3:4], bias[:], AX.X, ALU.add))
            link(dve.tensor_scalar(wmean[:], wmean[:], 1.0 / D, None, ALU.mult))
            for c in range(3):
                dve.tensor_scalar(w[:, c, :], w[:, c, :], wmean[:, c:c + 1], None, ALU.subtract)
            dve.tensor_scalar(bias[:], bias[:], wmean[:, 3:4], None, ALU.subtract)
            dve.wait_ge(con_in, 16)
            dve.tensor_copy(tri_h[:], con[:, C_TRI:C_TRI + P])
            dve.tensor_copy(ident_h[:], ident).then_inc(weights_ready, 1)
            dve.wait_ge(weights_ready, 1)

            dve.wait_ge(ids_in, 16 * 6)
            link(dve.tensor_copy(ids_f, ids_i))
            link(dve.tensor_scalar(ids_i[:, 0, :], ids_i[:, 1, :], P - 1, None, ALU.bitwise_and))
            dve.tensor_copy(low_h[:], ids_i[:, 0, :])
            link(dve.tensor_tensor(high_h[:], ids_i[:, 1, :], ids_i[:, 0, :], ALU.subtract))
            df = ids_f[:, 1, :].rearrange("p (s e) -> p s e", s=2)
            dve.tensor_reduce(span[:, 0, :], df, AX.X, ALU.min)
            link(dve.tensor_reduce(span[:, 1, :], df, AX.X, ALU.max))
            link(dve.tensor_scalar(span[:, 2, :], span[:, 0, :], float(WIN_MAX), None, ALU.min))
            link(dve.tensor_tensor(span[:, 3, :], span[:, 1, :], span[:, 2, :], ALU.subtract))
            link(dve.tensor_scalar(span[:, 3, :], span[:, 3, :], float(P), None, ALU.is_ge))
            link(dve.scalar_tensor_tensor(span[:, 1, :], span[:, 3, :], -4.0 * NPAD, span[:, 2, :], ALU.mult, ALU.add))
            for n, at in enumerate((1, 2, 3)):
                for s in range(2):
                    ins = dve.tensor_scalar(diag[:, n, s, :], ident, span[:, at, s:s + 1], None, ALU.mult)
            link(ins)
            dve.nop().then_inc(ids_split, 1)
            for n, to in enumerate((src_i, dst_i)):
                for s in range(2):
                    dve.wait_ge(cols_turned, 2 * n + s + 1)
                    dve.tensor_copy(to[:, :, s, :], pH[s][:, :, 0:PAIRS].rearrange("p k q -> p q k")).then_inc(cols_read, 1)
            dve.wait_ge(cols_read, 4)
            dve.wait_ge(spans_spread, 1)
            dve.tensor_scalar(win_f[:], pM[:, 0:2, 0:PAIRS].rearrange("p s q -> p q s"), iota, None, ALU.add)
            dve.tensor_copy(win_i[:].rearrange("p (q s) -> p q s", s=2), pM[:, 2:4, 0:PAIRS].rearrange("p s q -> p q s"))
            dve.wait_ge(clear_set, 2)
            for n, skip in enumerate((0, 3)):
                ins = dve.tensor_copy(flags[:, n, skip:skip + 2 * PAIRS].rearrange("p (q s) -> p q s", s=2),
                                      pT[:, 0:2, 0:PAIRS].rearrange("p s q -> p q s"))
            link(ins)
            dve.nop().then_inc(windows_ready, 1)
            link(dve.tensor_scalar(low_c, src_i[:], P - 1, None, ALU.bitwise_and))
            dve.tensor_scalar(place[:], low_c, 1.0, None, ALU.add)
            link(dve.tensor_tensor(src_i[:], src_i[:], low_c, ALU.subtract))
            link(dve.tensor_scalar(block_h[:], src_i[:].rearrange("p q s k -> p (q s k)"), 1.0 / P, 1.0, ALU.mult, ALU.add))
            with dve.Fori(0, CHUNKS) as i:
                for j in range(CH):
                    dve.tensor_scalar(member[:, bass.ds(i * CH + j, 1), :].rearrange("p a t -> p (a t)"), block_h[:],
                                      con[:, bass.ds(i * CH + j + C_ROW, 1)], None, ALU.is_equal, ALU.add,
                                      accum_out=count_p[:, bass.ds(i * CH + j, 1)]).then_inc(members_ready, 1)

            dve.wait_ge(counted, 1)
            link(dve.tensor_scalar(count_i[:, 0, :], pR[:, 0:BLOCKS], float(RUN - 1), None, ALU.add))
            link(dve.tensor_scalar(count_i[:, 1, :], count_i[:, 0, :], RUN.bit_length() - 1, None, ALU.logical_shift_right))
            link(dve.tensor_copy(runs[:], count_i[:, 1, :]))
            link(dve.tensor_tensor_scan(ends[:], ones[:, 0:BLOCKS], runs[:], 0.0, ALU.mult, ALU.add))
            link(dve.tensor_tensor(fill_a[:], ends[:], runs[:], ALU.subtract))
            link(dve.tensor_scalar(free_row[:], fill_a[0:1, :], float(RUN), None, ALU.mult))
            link(dve.tensor_scalar(fill_a[:], ends[:], float(RUN), -float(RUN), ALU.mult, ALU.add))
            link(dve.tensor_scalar(fill_b[:], con[:, C_ROW:C_ROW + BLOCKS], float(RUN), float(CLEAR * RUN), ALU.mult, ALU.add))
            link(dve.tensor_tensor(fill_b[:], fill_b[:], fill_a[:], ALU.subtract))
            link(dve.scalar_tensor_tensor(fill_b[:], runs[:], 0.0, fill_b[:], ALU.is_equal, ALU.mult))
            dve.tensor_tensor(fill_i[:, 0:BLOCKS], fill_a[:], fill_b[:], ALU.add).then_inc(fills_ready, 1)
            for i in range(4):
                ins = dve.tensor_scalar(past_end[:, i, :], ends[:], con[:, C_RUN + i:C_RUN + i + 1], None, ALU.is_le)
            link(ins)
            link(dve.tensor_reduce(run_cols[:, 2, :], past_end[:], AX.X, ALU.add))
            link(dve.tensor_scalar(run_cols[:, 0, :], run_cols[:, 2, :], BLOCKS - 1.0, None, ALU.min))
            link(dve.tensor_scalar(run_cols[:, 2, :], run_cols[:, 2, :], float(BLOCKS), None, ALU.is_ge))
            number = con[:, C_RUN:C_RUN + 4]
            link(dve.tensor_scalar(run_cols[:, 1, :], number, -float(RUN), float(CLEAR * RUN), ALU.mult, ALU.add))
            link(dve.tensor_tensor(run_cols[:, 1, :], run_cols[:, 1, :], run_cols[:, 2, :], ALU.mult))
            dve.scalar_tensor_tensor(run_cols[:, 1, :], number, float(RUN), run_cols[:, 1, :], ALU.mult, ALU.add
                                     ).then_inc(runs_found, 1)
            dve.wait_ge(runs_turned, 1)
            dve.memset(sched[:, 0, 0:8], 0)
            dve.memset(sched[:, 0, 8 + 4 * P:], 0)
            dve.tensor_copy(sched[:, 0, 8:8 + 4 * P], pX[0:1, :, :].rearrange("a k j -> a (k j)"))
            dve.tensor_copy(sched[:, 1, 8:8 + 4 * P], pR[0:1, :]).then_inc(sched_ready, 1)
            dve.wait_ge(sched_ready, 1)

            def place_rows(q, s):
                g = 4 * q + s
                dve.wait_ge(free_found, g + 1)
                dve.tensor_copy(free_row[:], next_rows[0:1, TILES, :]).then_inc(free_kept, 1)
                if past(g, 1):
                    dve.wait_ge(row_found, g)
                dve.tensor_tensor(chosen[:], next_rows[:, 0:TILES, :],
                                  member[:, :, bass.ds(g * TILES, TILES)].rearrange("p b k -> p k b"),
                                  ALU.mult).then_inc(chosen_ready, 1)
                dve.wait_ge(chosen_ready, g + 1)
                if past(g, 1):
                    dve.wait_ge(row_ready, g)
                dve.tensor_reduce(row_f[:], chosen[:], AX.X, ALU.add).then_inc(row_found, 1)
                dve.wait_ge(row_found, g + 1)
                if past(q, 1):
                    dve.wait_ge(sorted_out[s], 16 * TILES * q)
                dve.tensor_copy(row_now[s][:], row_f[:]).then_inc(row_ready, 1)

            def build(q, s):
                g, pair, h = 4 * q + s, 2 * q + s // 2, s % 2
                dve.wait_ge(dst_spread, g + 1)
                if past(g, 2):
                    dve.wait_ge(h_ready, g - 1)
                dve.tensor_scalar(hot[:, h, :, :], pD[:].rearrange("p (j k) -> p k j", k=TILES),
                                  win_f[:, bass.ds(pair, 1), h], None, ALU.is_equal).then_inc(hot_built, 1)

            def ids(q, s):
                g = 4 * q + s
                if past(g, 2):
                    dve.wait_ge(settled, g - 1)
                dve.tensor_copy(dst_now[s % 2][:], column(dst_i, q, s)).then_inc(gather_ready, 1)

            load_flags = registers(dve, "apart", 4)
            outside = []

            def flags_of(q):
                outside[:] = load_flags(flags[:, 0, :], 4 * q, 1)

            def keep_rows(q, s):
                g, h = 4 * q + s, s % 2
                if past(q, 1):
                    dve.wait_ge(sorted_out[s], 16 * TILES * q)
                dve.tensor_copy(zrow[:, s, :, D:D + 1].rearrange("p k a -> p (k a)"), column(place, q, s))
                with dve.If(outside[s]):
                    dve.wait_ge(h_ready, g + 1)
                    dve.wait_ge(settled, g + 1)
                    dve.tensor_tensor(zrow[:, s, :, 0:D], pH[h][:], gat[:, h, :, :], ALU.add).then_inc(rows_kept, 1)
                with dve.Else():
                    dve.wait_ge(h_ready, g + 1)
                    dve.tensor_copy(zrow[:, s, :, 0:D], pH[h][:]).then_inc(rows_kept, 1)

            def first_step(q, s):
                nxt = shift(q, s, 1, QUADS, 4)
                if nxt:
                    build(*nxt)
                    ids(*nxt)
                keep_rows(q, s)
                if nxt:
                    place_rows(*nxt)

            for slot in range(2):
                dve.wait_ge(xb_out[slot], 16 * ((CHUNKS + 1 - slot) // 2))
            ids(0, 0)
            build(0, 0)
            place_rows(0, 0)
            run_quads(dve, first_step, flags_of)

            def join(q, s):
                g, r = 8 * q + s, s % 4
                dve.wait_ge(z_in[r], 32 * (2 * q + s // 4 + 1))
                dve.wait_ge(xa_picked, g + 1)
                rest = h_bank[r][:, JOINED:, :]
                dve.tensor_tensor(rest, rest, zrow[:, r, JOINED:, 0:D], ALU.add).then_inc(h2_ready, 1)

            def invert(q, s):
                g, r = 8 * q + s, s % 4
                dve.wait_ge(std_ready, g + 1)
                dve.reciprocal(rstd[:, r, :], std[:, r, :]).then_inc(rstd_ready, 1)

            def scale(q, s):
                g, r = 8 * q + s, s % 4
                dve.wait_ge(rstd_ready, g + 1)
                for k in range(TILES):
                    ins = dve.scalar_tensor_tensor(h_bank[r][:, k, :], h_bank[r][:, k, :], rstd[:, r, k:k + 1], gamma_b[:],
                                                   ALU.mult, ALU.mult)
                ins.then_inc(scaled, 1)

            def add_beta(q, s):
                g, r = 8 * q + s, s % 4
                dve.wait_ge(scaled, g + 1)
                dve.tensor_tensor(h_bank[r], h_bank[r], beta_b[:].unsqueeze(1).to_broadcast([P, TILES, D]), ALU.add
                                  ).then_inc(shifted, 1)

            def add_sums(q, s, u):
                g = 8 * q + s
                dve.wait_ge(summed, g + 1)
                at = dve.snap(into[2 * ((s + 4) % 8) + u], min_val=0, max_val=BLOCKS - 1)
                rows = total[:, bass.ds(at, 1), :].rearrange("p a d -> p (a d)")
                if past(g, 1) or u:
                    dve.wait_ge(added, 2 * g + u)
                dve.tensor_tensor(rows, sum_bank[s % 2][:, u, :], rows, ALU.add).then_inc(added, 1)

            into = [dve.alloc_register(f"into{i}") for i in range(16)]

            def blocks_of(q):
                dve.load(into, sched[0:1, 0, bass.ds(16 * q, 16)])

            def second_step(q, s):
                last, old = shift(q, s, -1, OCTS, 8), shift(q, s, -4, OCTS, 8)
                if last:
                    invert(*last)
                if old:
                    add_sums(*old, 0)
                join(q, s)
                if last:
                    scale(*last)
                if old:
                    add_sums(*old, 1)
                if s == 7:
                    blocks_of(q + 1)
                if last:
                    add_beta(*last)

            dve.wait_ge(total_in, 32)
            blocks_of(0)
            run_octs(dve, second_step)
            invert(OCTS - 1, 7)
            scale(OCTS - 1, 7)
            add_beta(OCTS - 1, 7)
            for s in range(4, 8):
                for u in range(2):
                    add_sums(OCTS - 1, s, u)
            dve.wait_ge(added, RUNS)

            for c in range(CHUNKS + 1):
                if c < CHUNKS:
                    for j in range(c * CH, (c + 1) * CH):
                        ins = dve.bn_stats(stats[:, j, :], total[:, j, :])
                    link(ins)
                    for j in range(c * CH, (c + 1) * CH):
                        ins = dve.bn_aggr(moments[:, j, :], stats[:, j, :])
                    ins.then_inc(fin_var, 1)
                if c == 0:
                    continue
                js = slice((c - 1) * CH, c * CH)
                dve.wait_ge(fin_std, c)
                link(dve.reciprocal(rdev[:, js], sdev[:, js]))
                dve.scalar_tensor_tensor(offset[:, js], moments[:, js, 0], -1.0, rdev[:, js], ALU.mult, ALU.mult
                                         ).then_inc(fin_scale, 1)

        @block.scalar
        def _(act):
            def xT_copy(c, slot):
                for i, (a, z) in enumerate(BATCHES):
                    act.wait_ge(x_turned, 2 * c + i + 1)
                    act.copy(xT[:, i, 0:z - a, :], pH[i][:, 0:z - a, :]).then_inc(xT_copied, 1)

            def keep(c, slot):
                if past(c, 2):
                    act.wait_ge(xb_out[slot], 8 * (c - slot))
                for i, (a, z) in enumerate(BANKS):
                    act.wait_ge(node_done[i], c + 1)
                    got = node_bank[i][:, 0:(z - a) * 2 * D].rearrange("p (j n d) -> p j n d", n=2, d=D)
                    act.copy(xa[:, bass.ds(c * CH + a, z - a), :], got[:, :, 0, :])
                    act.copy(xb_now[:, slot, a:z, :], got[:, :, 1, :]).then_inc(node_kept[i], 1)

            def node_step(c, slot):
                xT_copy(c, slot)
                keep(c, slot)

            run_chunks(act, node_step)
            act.wait_ge(fills_ready, 1)
            clear_runs(act, "act_fill", FILLS_SP, FILLS_ACT, filled)

            def eaT_copy(q, s):
                g = 4 * q + s
                act.wait_ge(ea_turned, g + 1)
                if past(g, 2):
                    act.wait_ge(h_ready, g - 1)
                act.copy(eaT[:, s % 2, :, :], pT[:]).then_inc(eaT_copied, 1)

            run_quads(act, eaT_copy)

            def hot_copy(q, s):
                g, r = 8 * q + s, s % 4
                act.wait_ge(hotT_turned, g + 1)
                if past(g, 4):
                    act.wait_ge(xa_picked, g - 3)
                act.copy(hot2[:, r, :, :], turn_bank[s % 2]).then_inc(hot2_copied, 1)

            def deviation(q, s):
                g, r = 8 * q + s, s % 4
                act.wait_ge(h2_ready, g + 1)
                for k in range(TILES):
                    ins = act.activation(squared[:, s % 2, k, :], h_bank[r][:, k, :], ACT.Square,
                                         accum_out=squares[:, r, k:k + 1])
                ins.then_inc(squares_done, 1)
                act.wait_ge(squares_done, g + 1)
                act.activation(std[:, r, :], squares[:, r, :], ACT.Sqrt, bias=eps[:], scale=1.0 / D).then_inc(std_ready, 1)

            def relu(q, s):
                g, r = 8 * q + s, s % 4
                act.wait_ge(shifted, g + 1)
                if past(g, 4):
                    act.wait_ge(summed, g - 3)
                act.activation(msg[:, r, :, :], h_bank[r], ACT.Relu).then_inc(msg_ready, 1)

            def second_step(q, s):
                if shift(q, s, 1, OCTS, 8):
                    hot_copy(*shift(q, s, 1, OCTS, 8))
                deviation(q, s)
                if shift(q, s, -1, OCTS, 8):
                    relu(*shift(q, s, -1, OCTS, 8))

            hot_copy(0, 0)
            run_octs(act, second_step)
            relu(OCTS - 1, 7)

            for c in range(CHUNKS + 1):
                if c < CHUNKS:
                    act.wait_ge(fin_var, c + 1)
                    js = slice(c * CH, (c + 1) * CH)
                    act.activation(sdev[:, js], moments[:, js, 1], ACT.Sqrt, bias=eps[:], scale=1.0).then_inc(fin_std, 1)
                if c == 0:
                    continue
                d, slot = c - 1, (c - 1) % 2
                act.wait_ge(fin_scale, d + 1)
                if d >= 2:
                    act.wait_ge(stored[slot], 32 * (d // 2))
                for j in range(FIN_ACT):
                    at = d * CH + j
                    ins = act.activation(result[:, slot, j, :], total[:, at, :], ACT.Identity,
                                         bias=offset[:, at:at + 1], scale=rdev[:, at:at + 1])
                ins.then_inc(fin_done, 1)

        @block.tensor
        def _(pe):
            def node_step(c, slot):
                pe.wait_ge(x_in[slot], 16 * (c - slot) + 32)
                for i, (a, z) in enumerate(BATCHES):
                    if past(c, 1):
                        pe.wait_ge(xT_copied, 2 * c - 1 + i)
                    for j in range(a, z):
                        ins = pe.transpose(pH[i][:, j - a, :], x_now[:, slot, j, :], ident)
                    ins.then_inc(x_turned, 1)
                for m, (a, z) in enumerate(BANKS):
                    pe.wait_ge(xT_copied, 2 * c + (1 if z <= TILES else 2))
                    if past(c, 1):
                        pe.wait_ge(node_kept[m], c)
                    for j in range(a, z):
                        i = 0 if j < TILES else 1
                        to = node_bank[m][:, (j - a) * 2 * D:(j - a + 1) * 2 * D]
                        ins = pe.matmul(to, xT[:, i, j - BATCHES[i][0], :], w[:, 0:2, :].rearrange("p n d -> p (n d)"),
                                        start=True, stop=True)
                    ins.then_inc(node_done[m], 1)

            pe.wait_ge(weights_ready, 1)
            node_step(0, 0)
            pe.wait_ge(ids_split, 1)
            pe.wait_ge(xT_copied, 2)
            pe.wait_ge(node_kept[2], 1)
            pe.wait_ge(node_kept[3], 1)
            for n in range(2):
                for s in range(2):
                    if n:
                        pe.wait_ge(cols_read, s + 1)
                    ids = ids_f[0:PAIRS, n, s * GROUP:(s + 1) * GROUP].rearrange("q (p k) -> q k p", k=TILES)
                    for k in range(TILES):
                        ins = pe.transpose(pH[s][:, k, 0:PAIRS], ids[:, k, :], ident[0:PAIRS, 0:PAIRS])
                    ins.then_inc(cols_turned, 1)
            for n in range(3):
                for s in range(2):
                    to = (pM[:, 2 * n + s, 0:PAIRS] if n < 2 else pT[:, s, 0:PAIRS])
                    ins = pe.matmul(to, ones[0:PAIRS, :], diag[0:PAIRS, n, s, 0:PAIRS], start=True, stop=True)
            ins.then_inc(spans_spread, 1)
            pe.wait_ge(cols_read, 4)
            pe.wait_ge(windows_ready, 1)
            node_step(1, 1)
            with pe.Fori(1, CHUNKS // 2) as i:
                node_step(2 * i, 0)
                node_step(2 * i + 1, 1)

            pe.wait_ge(members_ready, BLOCKS)
            pe.matmul(pR[:, 0:BLOCKS], ones[:], count_p[:], start=True, stop=True).then_inc(counted, 1)
            node_step(CHUNKS - 1, 0)
            pe.wait_ge(runs_found, 1)
            for n, to in enumerate((pX[0:1, :, :].rearrange("a k j -> a (k j)"), pR[0:1, :])):
                for i in range(4):
                    ins = pe.matmul(to[:, i * P:(i + 1) * P], run_cols[:, n, i:i + 1], ident, start=True, stop=True)
            ins.then_inc(runs_turned, 1)
            pe.wait_ge(sched_ready, 1)
            for m in range(4):
                pe.wait_ge(node_kept[m], CHUNKS)

            def front(q, s):
                g, pair, h = 4 * q + s, 2 * q + s // 2, s % 2
                tail = isinstance(q, int) and g == 2 * PAIRS - 1 and TAIL % TILES
                if past(g, 1):
                    pe.wait_ge(hot_built, g)
                pick = ident_h[0:PAIRS, bass.ds(pair, 1)].to_broadcast([PAIRS, P])
                pe.matmul(pD[:], pick, high_h[0:PAIRS, h * GROUP:(h + 1) * GROUP], start=True, stop=False)
                pe.matmul(pD[:], pick, low_h[0:PAIRS, h * GROUP:(h + 1) * GROUP], start=False, stop=True
                          ).then_inc(dst_spread, 1)
                pe.wait_ge(ea_in[h], 16 * (pair + 2) if tail else 16 * (pair + 1))
                if past(g, 1):
                    pe.wait_ge(eaT_copied, g)
                for k in range(TILES):
                    ins = pe.transpose(pT[:, k, :], ea[:, h, k, :], ident)
                ins.then_inc(ea_turned, 1)

            def free_rows(q, s):
                g = 4 * q + s
                if past(g, 1):
                    pe.wait_ge(free_kept, g)
                    pe.wait_ge(chosen_ready, g)
                pe.matmul(next_rows, ones[0:1, :], free_row[:].unsqueeze(1).to_broadcast([1, TILES + 1, BLOCKS]),
                          start=True, stop=False, skip_group_check=True)
                for k in range(TILES):
                    mine = member[:, :, bass.ds(g * TILES + k, 1)].rearrange("p b a -> p a b")
                    pe.matmul(next_rows[:, k:k + 1, :], tri_h[:], mine, start=False, stop=False, skip_group_check=True)
                    ins = pe.matmul(next_rows[:, k + 1:TILES + 1, :], ones_h[:], mine.to_broadcast([P, TILES - k, BLOCKS]),
                                    start=False, stop=(k == TILES - 1), skip_group_check=True)
                ins.then_inc(free_found, 1)

            def products(q, s):
                g, pair, h = 4 * q + s, 2 * q + s // 2, s % 2
                pe.wait_ge(eaT_copied, g + 1)
                pe.wait_ge(hot_built, g + 1)
                pe.wait_ge(window_in[h], 16 * (pair + 1))
                if past(g, 2):
                    pe.wait_ge(rows_kept, g - 1)
                for k in range(TILES):
                    pe.matmul(pH[h][:, k, :], eaT[:, h, k, :], w[:, 2, :], start=True, stop=False)
                    ins = pe.matmul(pH[h][:, k, :], hot[:, h, k, :], window[:, h, :], start=False, stop=True)
                ins.then_inc(h_ready, 1)

            def first_step(q, s):
                nxt = shift(q, s, 1, QUADS, 4)
                products(q, s)
                if nxt:
                    front(*nxt)
                    free_rows(*nxt)

            free_rows(0, 0)
            front(0, 0)
            run_quads(pe, first_step)

            def turn_hot(q, s):
                g = 8 * q + s
                pe.wait_ge(hotT_built, g + 1)
                if past(g, 2):
                    pe.wait_ge(hot2_copied, g - 1)
                for k in range(TILES):
                    ins = pe.matmul(turn_bank[s % 2][:, k, :], hotT_h[:, s, k, :, 1], ident_h[:], start=True, stop=True)
                ins.then_inc(hotT_turned, 1)

            def pick_xa(q, s, at):
                g, r = 8 * q + s, s % 4
                if past(g, 4):
                    pe.wait_ge(msg_ready, g - 3)
                pe.matmul(h_bank[r][:, 0:JOINED, :], ident, zrow[:, r, 0:JOINED, 0:D], start=True, stop=False,
                          skip_group_check=True)
                pe.wait_ge(hot2_copied, g + 1)
                for u in range(2):
                    block_u = pe.snap(at[u], min_val=0, max_val=BLOCKS - 1)
                    for k in (2 * u, 2 * u + 1):
                        ins = pe.matmul(h_bank[r][:, k, :], hot2[:, r, k, :],
                                        xa[:, bass.ds(block_u, 1), :].rearrange("p a d -> p (a d)"), start=(k >= JOINED),
                                        stop=True, skip_group_check=True)
                ins.then_inc(xa_picked, 1)

            def sum_up(q, s):
                g, r = 8 * q + s, s % 4
                pe.wait_ge(msg_ready, g + 1)
                if past(g, 2):
                    pe.wait_ge(added, 2 * g - 2)
                for u in range(2):
                    for k in (2 * u, 2 * u + 1):
                        ins = pe.matmul(sum_bank[s % 2][:, u, :], hotT[:, s, k, :], msg[:, r, k, :], start=(k == 2 * u),
                                        stop=(k == 2 * u + 1))
                ins.then_inc(summed, 1)

            of = [pe.alloc_register(f"of{i}") for i in range(16)]

            def blocks_of(q):
                pe.load(of, sched[0:1, 0, bass.ds(16 * q + 8, 16)])

            def second_step(q, s):
                pick_xa(q, s, of[2 * s:2 * s + 2])
                if s == 7:
                    blocks_of(q + 1)
                if shift(q, s, 1, OCTS, 8):
                    turn_hot(*shift(q, s, 1, OCTS, 8))
                if shift(q, s, -3, OCTS, 8):
                    sum_up(*shift(q, s, -3, OCTS, 8))

            pe.wait_ge(rows_kept, 2 * PAIRS)
            pe.wait_ge(biased, CHUNKS)
            turn_hot(0, 0)
            blocks_of(0)
            run_octs(pe, second_step)
            for s in (5, 6, 7):
                sum_up(OCTS - 1, s)


def kernel(x, src, dst, edge_attr_128, L0_gnn_W, L0_gnn_b, L0_gnn_gamma, L0_gnn_beta):
    import numpy as _np
    import concourse.bacc as _bacc
    from concourse import mybir as _mybir
    from concourse.bass_utils import run_bass_kernel_spmd as _run

    named = {"x": x, "src": src, "dst": dst, "edge_attr": edge_attr_128, "W": L0_gnn_W, "b": L0_gnn_b,
             "gamma": L0_gnn_gamma, "beta": L0_gnn_beta, "consts": constants()}
    nc = _bacc.Bacc("TRN2", target_bir_lowering=False, num_devices=1)
    arrays, args = {}, []
    for name, a in named.items():
        a = _np.ascontiguousarray(a)
        arrays[f"in_{name}"] = a
        args.append(nc.dram_tensor(f"in_{name}", a.shape, _mybir.dt.from_np(a.dtype), kind="ExternalInput").ap())
    args.append(nc.dram_tensor("out_0", x.shape, _mybir.dt.float32, kind="ExternalOutput").ap())
    gnn_kernel(nc, *args)
    r = _run(nc, [arrays], core_ids=[0])
    return r.results[0]["out_0"]
```
